# Optimizing a Trainium2 kernel written in Bass

```python
import numpy as np
import jax
import jax.numpy as jnp

def _softmax(x, axis=-1):
    return jax.nn.softmax(x, axis=axis)

def _gelu(x):
    return jax.nn.gelu(x, approximate=True)

def _silu(x):
    return jax.nn.silu(x)

def _sigmoid(x):
    return jax.nn.sigmoid(x)

def _layernorm(x, axis=-1, eps=1e-05):
    m = jnp.mean(x, axis=axis, keepdims=True)
    v = jnp.var(x, axis=axis, keepdims=True)
    return (x - m) / jnp.sqrt(v + eps)

def _scatter_add(tgt, idx, src, axis=0):
    return tgt.at[idx].add(src)

def _segment_sum(src, seg, n):
    return jax.ops.segment_sum(src, seg, n)
kernel_name = 'mk_adaln_d1_jaxref_r8_2682d9'

def setup_inputs(seed: int=0):
    np.random.seed(seed)
    _w = jnp.asarray

    def _L0_attn_setup():
        import jax, jax.numpy as jnp
        import numpy as np
        DIM_IN, DIM_K, DIM_V, NH = (128, 128, 128, 16)
        DK, DV = (DIM_K // NH, DIM_V // NH)
        key = jax.random.key(seed)
        kx, kq, kk, kv = jax.random.split(key, 4)
        x = jax.random.normal(kx, (4, 256, DIM_IN), dtype=jnp.float32)
        Wq = jax.random.normal(kq, (DIM_K, DIM_IN), dtype=jnp.float32) / np.sqrt(DIM_IN)
        Wk = jax.random.normal(kk, (DK, DIM_IN), dtype=jnp.float32) / np.sqrt(DIM_IN)
        Wv = jax.random.normal(kv, (DV, DIM_IN), dtype=jnp.float32) / np.sqrt(DIM_IN)
        return {'x': x, 'Wq': Wq, 'Wk': Wk, 'Wv': Wv}
    _L0_attn_in = _L0_attn_setup()

    def _L0_ffn_setup():
        import jax, jax.numpy as jnp
        import numpy as np
        TOP_K = 2
        key = jax.random.key(seed)
        ks = jax.random.split(key, 6)
        B, T, H, E, F = (2, 256, 128, 8, 512)
        s = 0.02
        return {'hidden_states': jax.random.normal(ks[0], (B, T, H), dtype=jnp.float32), 'router_w': jax.random.normal(ks[1], (E, H), dtype=jnp.float32) * s, 'w1': jax.random.normal(ks[2], (E, F, H), dtype=jnp.float32) * s, 'b1': jax.random.normal(ks[3], (E, F), dtype=jnp.float32) * s, 'w2': jax.random.normal(ks[4], (E, H, F), dtype=jnp.float32) * s, 'b2': jax.random.normal(ks[5], (E, H), dtype=jnp.float32) * s}
    _L0_ffn_in = _L0_ffn_setup()
    _L0_c = _w((lambda *s: np.random.randn(*s).astype(np.float32) * 0.05)(8, 128))
    _L0_wmod = _w((lambda *s: np.random.randn(*s).astype(np.float32) * 0.05)(128, 6 * 128) * 128 ** (-0.5))
    _d = {'L0_attn_x': _L0_attn_in['x'], 'L0_attn_Wq': _L0_attn_in['Wq'], 'L0_attn_Wk': _L0_attn_in['Wk'], 'L0_attn_Wv': _L0_attn_in['Wv'], 'L0_ffn_router_w': _L0_ffn_in['router_w'], 'L0_ffn_w1': _L0_ffn_in['w1'], 'L0_ffn_b1': _L0_ffn_in['b1'], 'L0_ffn_w2': _L0_ffn_in['w2'], 'L0_ffn_b2': _L0_ffn_in['b2'], 'L0_c': _L0_c, 'L0_wmod': _L0_wmod}
    _x0 = _d['L0_attn_x']
    _d['L0_attn_x'] = jax.random.normal(jax.random.fold_in(jax.random.key(seed), 1), (8, 512, 128), dtype=_x0.dtype)
    del _x0
    return _d

def reference(L0_attn_x, L0_attn_Wq, L0_attn_Wk, L0_attn_Wv, L0_ffn_router_w, L0_ffn_w1, L0_ffn_b1, L0_ffn_w2, L0_ffn_b2, L0_c, L0_wmod):

    def _L0_attn_ref(x, Wq, Wk, Wv):
        import jax, jax.numpy as jnp
        import numpy as np
        DIM_IN, DIM_K, DIM_V, NH = (128, 128, 128, 16)
        DK, DV = (DIM_K // NH, DIM_V // NH)
        B, S, _ = x.shape
        scale = 1.0 / np.sqrt(DK)
        q = (x @ Wq.T).reshape(B, S, NH, DK).transpose(0, 2, 1, 3)
        k = x @ Wk.T
        v = x @ Wv.T
        dist = jnp.einsum('bhqd,bkd->bhqk', q, k) * scale
        dist = jax.nn.softmax(dist, axis=-1)
        att = jnp.einsum('bhqk,bkd->bhqd', dist, v)
        return att.transpose(0, 2, 1, 3).reshape(B, S, DIM_V)

    def _L0_ffn_ref(hidden_states, router_w, w1, b1, w2, b2):
        import jax, jax.numpy as jnp
        import numpy as np
        TOP_K = 2
        x = hidden_states
        router_logits = jnp.einsum('bth,eh->bte', x, router_w)
        topk_values, topk_indices = jax.lax.top_k(router_logits, TOP_K)
        topk_weights = jax.nn.softmax(topk_values.astype(jnp.float32), axis=-1).astype(x.dtype)
        h1 = jnp.einsum('bth,efh->btef', x, w1) + b1
        h1 = jax.nn.gelu(h1, approximate=False)
        expert_outputs = jnp.einsum('btef,ehf->bteh', h1, w2) + b2
        gather_idx = topk_indices[..., None]
        topk_expert_outputs = jnp.take_along_axis(expert_outputs, gather_idx, axis=2)
        mixed_output = jnp.sum(topk_expert_outputs * topk_weights[..., None], axis=2)
        return mixed_output
    x = L0_attn_x
    mod = (_silu(L0_c) @ L0_wmod).reshape(L0_c.shape[0], 6, 1, -1)
    sa, ca, ga, sb, cb, gb = (mod[:, 0], mod[:, 1], mod[:, 2], mod[:, 3], mod[:, 4], mod[:, 5])
    ga = (2 * (ga >= 0) - 1) * jnp.maximum(jnp.abs(ga), 0.25)
    gb = (2 * (gb >= 0) - 1) * jnp.maximum(jnp.abs(gb), 0.25)
    h = _layernorm(x, axis=-1) * (1 + ca) + sa
    x = x + ga * _L0_attn_ref(h, L0_attn_Wq, L0_attn_Wk, L0_attn_Wv)
    h = _layernorm(x, axis=-1) * (1 + cb) + sb
    x = x + gb * _L0_ffn_ref(h, L0_ffn_router_w, L0_ffn_w1, L0_ffn_b1, L0_ffn_w2, L0_ffn_b2)
    return x

_drawn_inputs = setup_inputs


def setup_inputs(seed=0):
    import zlib

    import numpy as np

    out = dict(_drawn_inputs(seed))
    spreads = {}
    factors = {'L0_ffn_router_w': 6.366,
     'L0_ffn_w1': 6.052,
     'L0_ffn_b1': 8.0,
     'L0_ffn_w2': 5.951,
     'L0_ffn_b2': 8.0}
    for name, (base, spread) in spreads.items():
        noise = np.random.default_rng([zlib.crc32(name.encode()), seed]).standard_normal(out[name].shape)
        drawn = base * np.exp(spread * noise) if base else spread * noise
        out[name] = jnp.asarray(drawn.astype(out[name].dtype))
    for name, factor in factors.items():
        out[name] = (out[name] * factor).astype(out[name].dtype)
    return out
```

```python
import concourse.bass as bass
from concourse import mybir
from contextlib import ExitStack

FP32 = mybir.dt.float32
BF16 = mybir.dt.bfloat16
I32 = mybir.dt.int32
ALU = mybir.AluOpType
ACT = mybir.ActivationFunctionType
AX = mybir.AxisListType

B, S, D = 8, 512, 128
NH, DK = 16, 8
T = S // 128
NT = B * T
E, F = 8, 512
FC = F // 128
TS = 256
NST = (2 * B * S + E * (TS - 1)) // TS
G = 4
NG = NH // G
SCALE = DK ** -0.5
EPS = 1e-5
QUAD = 32


class Chain:

    def __init__(self, eng, sem, at=0, passed=None):
        self.eng, self.sem, self.at, self.passed = eng, sem, at, passed

    def link(self, ins):
        ins.then_inc(self.sem, 1)
        self.at = self.at + 1
        self.eng.wait_ge(self.sem, self.at)
        if self.passed:
            self.eng.sem_inc(self.passed, 1)


def split_in_three(own, whole, rest, part):
    own.link(own.eng.tensor_copy(part[:, 0, :], whole))
    own.link(own.eng.tensor_tensor(rest, whole, part[:, 0, :], ALU.subtract))
    own.link(own.eng.tensor_copy(part[:, 1, :], rest))
    own.link(own.eng.tensor_tensor(part[:, 2, :], rest, part[:, 1, :], ALU.subtract))


def adaln_block(nc, x, wq_t, wk_t, wv_t, router_t, w1_t, b1_t, w2_t, b2, c_t, wmod, constants, shift_rows, out):
    q_parts = nc.dram_tensor("q_parts", (B, 3, D, S), BF16, kind="Internal").ap()
    k_parts = nc.dram_tensor("k_parts", (B, 3 * DK, S), BF16, kind="Internal").ap()
    v_cols = nc.dram_tensor("v_cols", (B, 128, T * QUAD), FP32, kind="Internal").ap()

    x_sorted = nc.dram_tensor("x_sorted", (NST * TS, D), FP32, kind="Internal").ap()
    y_sorted = nc.dram_tensor("y_sorted", (NST * TS, D), FP32, kind="Internal").ap()
    out_rows = out.rearrange("b s d -> (b s) d")

    ctx = ExitStack()
    with ctx:
        def sb(name, shape, dt=FP32):
            return ctx.enter_context(nc.sbuf_tensor(name, shape, dt))

        def sem(name):
            return ctx.enter_context(nc.semaphore(name))

        X = sb("X", [128, NT, D])
        consts = sb("consts", [128, 3 * 128 + E + NST])
        ident, before, ones = (consts[:, 128 * n:128 * (n + 1)] for n in range(3))
        to_end, tile_number = consts[:, 3 * 128:3 * 128 + E], consts[:, 3 * 128 + E:]
        wq = sb("wq", [D, D])
        wk = sb("wk", [D, DK])
        wv = sb("wv", [D, DK])
        rw = sb("rw", [D, E])
        wm = sb("wm", [D, 6 * D])
        W1 = sb("W1", [128, E, F + FC])
        W2 = sb("W2", [128, E, FC, D])
        b2_row = sb("b2_row", [128, E, D])
        zero_row = sb("zero_row", [128, D])
        cT = sb("cT", [D, B])
        siluT = sb("siluT", [D, B])
        silu_den = sb("silu_den", [D, B])
        silu_wide = sb("silu_wide", [D, B, 128])
        mod_col = sb("mod_col", [D, 2, B])
        mod_row = sb("mod_row", [128, B, 4, D])
        GA, SB, CB, GB = range(4)
        eps = sb("eps", [128, 1])
        zero = sb("zero", [128, 1])

        ps = ctx.enter_context(nc.psum_tensor("ps", [128, 8 * 512], FP32))

        def bank(n, count=1):
            return ps[:, 512 * n:512 * (n + count)]

        loaded = sem("loaded")
        x_loaded = sem("x_loaded")
        experts_loaded = sem("experts_loaded")
        passed = sem("passed")
        dve_own = sem("dve_own")
        act_own = sem("act_own")
        pool_own = sem("pool_own")
        silu_exp = sem("silu_exp")
        silu_done = sem("silu_done")
        col_done = sem("col_done")
        row_done = sem("row_done")
        const_set = sem("const_set")
        guard_tmp = sb("guard_tmp", [128, 2, D * B])

        SETUP = 7 * 16
        ROW_ORDER = list(range(1, B)) + [0]

        with nc.Block() as block:
            @block.sync
            def _(eng):
                eng.dma_start(cT[:], c_t).then_inc(loaded, 16)
                eng.dma_start(wm[:], wmod).then_inc(loaded, 16)
                eng.dma_start(wq[:], wq_t).then_inc(loaded, 16)
                eng.dma_start(wk[:], wk_t).then_inc(loaded, 16)
                eng.dma_start(wv[:], wv_t).then_inc(loaded, 16)
                eng.dma_start(rw[:], router_t).then_inc(loaded, 16)
                eng.dma_start(consts[:], constants).then_inc(loaded, 16)
                eng.dma_start(W1[:, :, 0:F], w1_t).then_inc(experts_loaded, 16)
                eng.dma_start(W1[:, :, F:], b1_t).then_inc(experts_loaded, 16)
                eng.dma_start(W2[:], w2_t).then_inc(experts_loaded, 16)
                eng.dma_start(b2_row[:].rearrange("p e d -> p (e d)"), b2.rearrange("e d -> (e d)").partition_broadcast(128)).then_inc(experts_loaded, 16)
                eng.wait_ge(const_set, 3)
                eng.dma_start(x_sorted.rearrange("(p n) d -> p n d", p=128),
                              zero_row[:, None, :].to_broadcast([128, NST * TS // 128, D])).then_inc(experts_loaded, 16)
                eng.wait_ge(loaded, SETUP)
                eng.wait_ge(x_loaded, 16)

            @block.scalar
            def _(eng):
                eng.dma_start(X[:], x.rearrange("b (t p) d -> p (b t) d", p=128)).then_inc(x_loaded, 16)
                eng.wait_ge(loaded, SETUP)
                eng.wait_ge(const_set, 3)
                nc.scalar.activation(silu_den[:], cT[:], ACT.Exp, bias=zero[:], scale=-1.0).then_inc(silu_exp, 1)

            @block.vector
            def _(eng):
                own = Chain(eng, dve_own)
                eng.memset(eps[:], EPS).then_inc(const_set, 1)
                eng.memset(zero[:], 0.0).then_inc(const_set, 1)
                eng.memset(zero_row[:], 0.0).then_inc(const_set, 1)
                eng.wait_ge(silu_exp, 1)
                own.link(eng.tensor_scalar(silu_den[:], silu_den[:], 1.0, None, ALU.add))
                own.link(eng.reciprocal(silu_den[:], silu_den[:]))
                own.link(eng.tensor_tensor(siluT[:], silu_den[:], cT[:], ALU.mult))
                eng.tensor_copy(silu_wide[:], siluT[:, :, None].to_broadcast([D, B, 128])).then_inc(silu_done, 1)
                eng.wait_ge(col_done, 1)
                eng.tensor_copy(mod_col[:, 1, :], bank(0)[:, 0:B]).then_inc(dve_own, 1)
                own.at += 1
                own.link(eng.tensor_scalar(mod_col[:, 0, :], bank(0)[:, B:2 * B], 1.0, None, ALU.add))
                for n, b in enumerate(ROW_ORDER):
                    eng.wait_ge(row_done, n + 1)
                    eng.tensor_copy(mod_row[:, b, :, :], bank(b)).then_inc(dve_own, 1)
                    own.at += 1
                eng.wait_ge(dve_own, own.at)
                own.link(eng.tensor_scalar(mod_row[:, :, CB, :], mod_row[:, :, CB, :], 1.0, None, ALU.add))
                for kind in (GA, GB):
                    g = mod_row[:, :, kind, :]
                    sign = guard_tmp[:, 0, :].rearrange("p (b d) -> p b d", b=B)
                    size = guard_tmp[:, 1, :].rearrange("p (b d) -> p b d", b=B)
                    own.link(eng.tensor_scalar(sign, g, 0.0, 2.0, ALU.is_ge, ALU.mult))
                    own.link(eng.tensor_scalar(size, g, -1.0, None, ALU.mult))
                    own.link(eng.tensor_tensor(size, size, g, ALU.max))
                    own.link(eng.tensor_scalar(size, size, 0.25, None, ALU.max))
                    own.link(eng.scalar_tensor_tensor(g, sign, 1.0, size, ALU.subtract, ALU.mult))

            @block.tensor
            def _(eng):
                eng.wait_ge(silu_done, 1)
                eng.wait_ge(loaded, SETUP)
                eng.matmul(bank(0)[:, 0:B], wm[:, 0:D], siluT[:], start=True, stop=True)
                eng.matmul(bank(0)[:, B:2 * B], wm[:, D:2 * D], siluT[:], start=True, stop=True).then_inc(col_done, 1)
                for b in ROW_ORDER:
                    if b == 0:
                        eng.wait_ge(dve_own, 5)
                    eng.matmul(bank(b), silu_wide[:, b, :], wm[:, 2 * D:6 * D], start=True, stop=True).then_inc(row_done, 1)


        with ExitStack() as c1:
            def sb1(name, shape, dt=FP32):
                return c1.enter_context(nc.sbuf_tensor(name, shape, dt))

            stats = [sb1(f"stats{p}", [128, T, 6]) for p in (0, 1)]
            mean_var = [sb1(f"mean_var{p}", [128, T, 2]) for p in (0, 1)]
            rstd = [sb1(f"rstd{p}", [128, T]) for p in (0, 1)]
            xn = [sb1(f"xn{p}", [128, T, D]) for p in (0, 1)]
            hT = [sb1(f"hT{p}", [D, S]) for p in (0, 1)]
            qk = [sb1(f"qk{p}", [D, 2, S]) for p in (0, 1)]
            rest = [sb1(f"rest{p}", [D, 2, S]) for p in (0, 1)]
            parts = [sb1(f"parts{p}", [D, 2, 3, S], BF16) for p in (0, 1)]
            vcol = [sb1(f"vcol{p}", [128, T, QUAD]) for p in (0, 1)]
            ln_own, std_done, xn_done, xT_done, hT_done = (sem(n) for n in ("ln_own", "std_done", "xn_done", "xT_done", "hT_done"))
            proj_done, qk_copied, v_set, v_copied, split_own = (sem(n) for n in ("proj_done", "qk_copied", "v_set", "v_copied", "split_own"))
            stored = [sem(f"stored{p}") for p in (0, 1)]
            LN_OPS = 2 * T + 2
            SPLIT_OPS = 8

            with nc.Block() as block:
                @block.vector
                def _(eng):
                    for p in (0, 1):
                        eng.memset(vcol[p][:], 0.0).then_inc(v_set, 1)
                    eng.wait_ge(v_set, 2)
                    for p in (0, 1):
                        eng.memset(vcol[p][:, :, DK:DK + 1], 1.0).then_inc(v_set, 1)

                    def tile_of(b, t):
                        return X[:, bass.ds(b * T + t, 1), :].rearrange("p a d -> p (a d)")

                    def normalize(i, p):
                        b = i * 2 + p
                        own = Chain(eng, ln_own, b * LN_OPS)
                        eng.wait_ge(xn_done, i * (2 * T))
                        for t in range(T):
                            eng.bn_stats(stats[p][:, t, :], tile_of(b, t)).then_inc(ln_own, 1)
                        eng.wait_ge(ln_own, b * LN_OPS + T)
                        eng.sem_inc(passed, 1)
                        for t in range(T):
                            eng.bn_aggr(mean_var[p][:, t, :], stats[p][:, t, :]).then_inc(ln_own, 1)
                        eng.wait_ge(ln_own, b * LN_OPS + 2 * T)
                        eng.tensor_copy(rstd[p][:], mean_var[p][:, :, 1]).then_inc(ln_own, 1)
                        eng.wait_ge(std_done, b + 1)
                        eng.reciprocal(rstd[p][:], rstd[p][:]).then_inc(ln_own, 1)
                        eng.wait_ge(ln_own, (b + 1) * LN_OPS)
                        eng.wait_ge(xT_done, i * 2)
                        for t in range(T):
                            eng.tensor_scalar(xn[p][:, t, :], tile_of(b, t), mean_var[p][:, t, 0:1], rstd[p][:, t:t + 1],
                                              ALU.subtract, ALU.mult).then_inc(xn_done, 1)

                    def values(i, p):
                        b = i * 2 + p
                        eng.wait_ge(proj_done, b + 1)
                        eng.wait_ge(stored[p], i * 48)
                        eng.wait_ge(v_set, 4)
                        eng.tensor_copy(vcol[p][:, :, 0:DK],
                                        bank(4 * p + 3)[:, 0:T * DK].rearrange("p (t d) -> p t d", t=T)).then_inc(v_copied, 1)

                    with eng.Fori(0, B // 2) as i:
                        normalize(i, 0)
                        normalize(i, 1)
                        values(i, 0)
                        values(i, 1)

                @block.scalar
                def _(eng):
                    def root(i, p):
                        b = i * 2 + p
                        eng.wait_ge(ln_own, b * LN_OPS + 2 * T + 1)
                        nc.scalar.activation(rstd[p][:], rstd[p][:], ACT.Sqrt, bias=eps[:]).then_inc(std_done, 1)

                    def batch(i, p):
                        b = i * 2 + p
                        eng.wait_ge(xT_done, b + 1)
                        eng.wait_ge(proj_done, i * 2)
                        nc.scalar.activation(hT[p][:], bank(4 * p), ACT.Identity, bias=mod_col[:, 1, bass.ds(b, 1)],
                                             scale=mod_col[:, 0, bass.ds(b, 1)]).then_inc(hT_done, 1)
                        eng.wait_ge(proj_done, b + 1)
                        eng.wait_ge(split_own, i * (2 * SPLIT_OPS))
                        nc.scalar.copy(qk[p][:, 0, :], bank(4 * p + 1)).then_inc(qk_copied, 1)
                        nc.scalar.copy(qk[p][0:DK, 1, :], bank(4 * p + 2)[0:DK, :]).then_inc(qk_copied, 1)

                    with eng.Fori(0, B // 2) as i:
                        root(i, 0)
                        root(i, 1)
                        batch(i, 0)
                        batch(i, 1)

                @block.tensor
                def _(eng):
                    def batch(i, p):
                        b = i * 2 + p
                        eng.wait_ge(xn_done, (b + 1) * T)
                        eng.wait_ge(hT_done, i * 2)
                        for t in range(T):
                            ins = eng.transpose(bank(4 * p)[:, 128 * t:128 * (t + 1)], xn[p][:, t, :], ident)
                        ins.then_inc(xT_done, 1)
                        eng.wait_ge(hT_done, b + 1)
                        eng.wait_ge(qk_copied, i * 4)
                        eng.wait_ge(v_copied, i * 2)
                        eng.matmul(bank(4 * p + 1), wq[:], hT[p][:], start=True, stop=True)
                        eng.matmul(bank(4 * p + 2)[0:DK, :], wk[:], hT[p][:], start=True, stop=True)
                        for t in range(T):
                            ins = eng.matmul(bank(4 * p + 3)[:, DK * t:DK * (t + 1)], hT[p][:, 128 * t:128 * (t + 1)], wv[:],
                                             start=True, stop=True)
                        ins.then_inc(proj_done, 1)

                    with eng.Fori(0, B // 2) as i:
                        batch(i, 0)
                        batch(i, 1)

                @block.gpsimd
                def _(eng):
                    def batch(i, p):
                        b = i * 2 + p
                        own = Chain(eng, split_own, b * SPLIT_OPS, passed)
                        eng.wait_ge(qk_copied, b * 2 + 2)
                        eng.wait_ge(stored[p], i * 48)
                        eng.sem_inc(passed, 1)
                        for n, rows in ((0, D), (1, DK)):
                            split_in_three(own, qk[p][0:rows, n, :], rest[p][0:rows, n, :], parts[p][0:rows, n, :, :])

                    with eng.Fori(0, B // 2) as i:
                        batch(i, 0)
                        batch(i, 1)

                @block.sync
                def _(eng):
                    def batch(i, p):
                        b = i * 2 + p
                        eng.wait_ge(split_own, (b + 1) * SPLIT_OPS)
                        eng.dma_start(q_parts[bass.ds(b, 1), :, :, :].rearrange("a i p t -> p (a i) t"),
                                      parts[p][:, 0, :, :]).then_inc(stored[p], 16)
                        eng.dma_start(k_parts[bass.ds(b, 1), :, :].rearrange("a (i p) t -> p (a i) t", p=DK),
                                      parts[p][0:DK, 1, :, :]).then_inc(stored[p], 16)
                        eng.wait_ge(v_copied, b + 1)
                        eng.dma_start(v_cols[bass.ds(b, 1), :, :].rearrange("a p c -> (a p) c"),
                                      vcol[p][:].rearrange("p t c -> p (t c)")).then_inc(stored[p], 16)

                    with eng.Fori(0, B // 2) as i:
                        batch(i, 0)
                        batch(i, 1)
                    for p in (0, 1):
                        eng.wait_ge(stored[p], B // 2 * 48)

        with ExitStack() as c2:
            def sb2(name, shape, dt=FP32):
                return c2.enter_context(nc.sbuf_tensor(name, shape, dt))

            Q = [sb2(f"Q{p}", [128, NH, S], BF16) for p in (0, 1)]
            KM = [sb2(f"KM{p}", [128, S], BF16) for p in (0, 1)]
            KS = [sb2(f"KS{p}", [128, S], BF16) for p in (0, 1)]
            V = [sb2(f"V{p}", [128, T, QUAD]) for p in (0, 1)]
            P = [sb2(f"P{p}", [128, G, S]) for p in (0, 1)]
            neg_max = [sb2(f"neg_max{p}", [128, G * T]) for p in (0, 1)]
            neg_max_T = [sb2(f"neg_max_T{p}", [G * T, 128]) for p in (0, 1)]
            max_rest = [sb2(f"max_rest{p}", [G * T, 128]) for p in (0, 1)]
            max_parts = [sb2(f"max_parts{p}", [G * T, 3, 128], BF16) for p in (0, 1)]
            att_u = [sb2(f"att_u{p}", [128, S]) for p in (0, 1)]
            recip = [sb2(f"recip{p}", [128, T, G]) for p in (0, 1)]
            att = [sb2(f"att{p}", [128, T, D]) for p in (0, 1)]
            gated = sb2("gated", [128, T, D])
            RING = G * T + 1
            X1_OPS = T + 1
            GP = 2 * NG
            LOADS = 9 + 3 + 3 + 1
            op_set, max_ring, ring_used, score_done, exp_done, pv_done, att_out, att_T, att_norm, recip_done = (
                sem(n) for n in ("op_set", "max_ring", "ring_used", "score_done", "exp_done", "pv_done", "att_out", "att_T",
                                 "att_norm", "recip_done"))
            max_split, x1_own = sem("max_split"), sem("x1_own")
            batch_loaded = [sem(f"batch_loaded{p}") for p in (0, 1)]
            shift_loaded = [sem(f"shift_loaded{p}") for p in (0, 1)]

            with nc.Block() as block:
                @block.vector
                def _(eng):
                    for p in (0, 1):
                        eng.memset(Q[p][:], 0.0).then_inc(op_set, 1)
                        eng.memset(KM[p][:], 0.0).then_inc(op_set, 1)
                        eng.memset(KS[p][:], 0.0).then_inc(op_set, 1)

                @block.sync
                def _(eng):
                    eng.wait_ge(op_set, 6)
                    for p in (0, 1):
                        for blk in range(3):
                            eng.dma_start(KS[p][QUAD * blk + 24:QUAD * blk + 32, :], shift_rows).then_inc(op_set, 16)
                    eng.wait_ge(op_set, 6 + 6 * 16)

            with nc.Block() as block:
                @block.sync
                def _(eng):
                    def load(b, p):
                        for blk in range(3):
                            for r in range(3):
                                at = QUAD * blk + DK * r
                                eng.dma_start(Q[p][at:at + DK, :, :],
                                              q_parts[bass.ds(b, 1), blk, :, :].rearrange("a (h d) t -> d (a h) t", d=DK)
                                              ).then_inc(batch_loaded[p], 16)
                            at = QUAD * blk
                            for K in (KM[p], KS[p]):
                                eng.dma_start(K[at:at + 3 * DK, :],
                                              k_parts[bass.ds(b, 1), :, :].rearrange("a p t -> (a p) t")).then_inc(batch_loaded[p], 16)
                        eng.dma_start(V[p][:].rearrange("p t c -> p (t c)"),
                                      v_cols[bass.ds(b, 1), :, :].rearrange("a p c -> (a p) c")).then_inc(batch_loaded[p], 16)

                    def shift(n_split, m):
                        p, h = (m // NG) % 2, (m % NG) * G
                        eng.wait_ge(max_split, n_split)
                        for blk in range(3):
                            at = QUAD * blk + 24
                            eng.dma_start(Q[p][at:at + 1, h:h + G, :], max_parts[m % 2][:, blk, :]).then_inc(shift_loaded[m % 2], 16)

                    def turn(i, last):
                        for m in range(GP):
                            if not (last and m == GP - 1):
                                shift((i * GP + m + 2) * 4, m + 1)
                            if m == NG and not last:
                                eng.wait_ge(pv_done, i * (GP * T) + NG * T + 2)
                                load(i * 2 + 2, 0)
                            if m == GP - 1 and not last:
                                eng.wait_ge(pv_done, (i + 1) * (GP * T) + 2)
                                load(i * 2 + 3, 1)

                    load(0, 0)
                    load(1, 1)
                    shift(4, 0)
                    with eng.Fori(0, B // 2 - 1) as i:
                        turn(i, False)
                    turn(B // 2 - 1, True)

                @block.tensor
                def _(eng):
                    eng.sem_inc(pv_done, 2)

                    def maximum(ring, m, s, j):
                        eng.wait_ge(ring_used, ring + 1)
                        eng.matmul(bank(4 + ring_parity[0] % 2), Q[(m // NG) % 2][:, (m % NG) * G + j, 128 * s:128 * (s + 1)],
                                   KM[(m // NG) % 2][:], start=True, stop=True).then_inc(max_ring, 1)
                        ring_parity[0] += 1

                    def turn_maxima(ring, m):
                        eng.wait_ge(ring_used, ring + 2)
                        eng.transpose(bank(4 + ring_parity[0] % 2)[0:G * T, 0:128], neg_max[m % 2][:], ident).then_inc(max_ring, 1)
                        ring_parity[0] += 1

                    def scores(i, m, s, u):
                        p = (m // NG) % 2
                        if s == 0 and u == 0:
                            eng.wait_ge(shift_loaded[m % 2], (i * (GP // 2) + m // 2 + 1) * 48)
                        eng.wait_ge(exp_done, i * (GP * T * 2) + (m * T + s) * 2 + u + 1)
                        for j in range(2):
                            ins = eng.matmul(bank(2 * u + j), KS[p][:, 128 * s:128 * (s + 1)], Q[p][:, (m % NG) * G + 2 * u + j, :],
                                             start=True, stop=True)
                        ins.then_inc(score_done, 1)

                    def values(i, m, s, heads):
                        if heads[0] == 0:
                            eng.wait_ge(exp_done, i * (GP * T * 2) + (m * T + s) * 2 + 4)
                            if s == 0:
                                eng.wait_ge(att_norm, i * GP + m + 1)
                        for j in heads:
                            ins = eng.matmul(bank(6 + m % 2)[QUAD * j:QUAD * (j + 1), :], V[(m // NG) % 2][:, s, :], P[s % 2][:, j, :],
                                             start=(s == 0), stop=(s == T - 1), tile_position=(0, QUAD * j))
                        if heads[-1] == G - 1:
                            ins.then_inc(pv_done, 1)

                    def back(i, m):
                        eng.wait_ge(att_out, i * GP + m + 1)
                        for t in range(T):
                            ins = eng.transpose(bank(6 + m % 2)[:, 128 * t:128 * (t + 1)], att_u[m % 2][:, 128 * t:128 * (t + 1)],
                                                ident)
                        ins.then_inc(att_T, 1)

                    def turn(i, last):
                        ring = i * (GP * RING) + 2 * G * T + 1
                        for m in range(GP):
                            for s in range(T):
                                if s == 1 and not (last and m == GP - 1):
                                    turn_maxima(ring, m + 1)
                                    ring = ring + 1
                                ahead = not (last and m >= GP - 2)
                                if ahead and m == NG - 2 and s == 0:
                                    eng.wait_ge(batch_loaded[1], (i + 1) * (16 * LOADS))
                                if ahead and m == GP - 2 and s == 0:
                                    eng.wait_ge(batch_loaded[0], (i + 2) * (16 * LOADS))
                                for j in range(G):
                                    if ahead:
                                        maximum(ring, m + 2, s, j)
                                        ring = ring + 1
                                    if j % 2 == 0:
                                        scores(i, m, s, j // 2)
                                    elif s > 0:
                                        values(i, m, s - 1, (j - 1, j))
                                    elif m > 0:
                                        values(i, m - 1, T - 1, (j - 1, j))
                                if s == 2 and m > 0:
                                    back(i, m - 1)
                        values(i, GP - 1, T - 1, range(G))
                        back(i, GP - 1)

                    ring_parity = [0]
                    eng.wait_ge(batch_loaded[0], 16 * LOADS)
                    for n in range(2 * G * T):
                        maximum(n, n // (G * T), n // G % T, n % G)
                    turn_maxima(2 * G * T, 0)
                    with eng.Fori(0, B // 2 - 1) as i:
                        turn(i, False)
                    turn(B // 2 - 1, True)

                @block.scalar
                def _(eng):
                    eng.sem_inc(exp_done, 2)

                    def out_of_bank(i, m):
                        eng.wait_ge(pv_done, i * (GP * T) + (m + 1) * T + 2)
                        nc.scalar.copy(att_u[m % 2][:], bank(6 + m % 2)).then_inc(att_out, 1)

                    def turn(i):
                        for m in range(GP):
                            for s in range(T):
                                eng.wait_ge(pv_done, i * (GP * T) + m * T + s + 1)
                                for u in range(2):
                                    eng.wait_ge(score_done, i * (GP * T * 2) + (m * T + s) * 2 + u + 1)
                                    nc.scalar.activation(P[s % 2][:, 2 * u:2 * u + 2, :],
                                                         bank(2 * u, 2).rearrange("p (j t) -> p j t", j=2),
                                                         ACT.Exp, bias=zero[:], scale=SCALE).then_inc(exp_done, 1)
                                if s == 0 and m > 0:
                                    out_of_bank(i, m - 1)
                        out_of_bank(i, GP - 1)

                    with eng.Fori(0, B // 2) as i:
                        turn(i)

                @block.vector
                def _(eng):
                    eng.sem_inc(ring_used, 2)
                    eng.sem_inc(att_norm, 2)
                    ring_parity = [0]

                    def maxima(ring, m, s):
                        for j in range(G):
                            eng.wait_ge(max_ring, ring + j + 1)
                            eng.tensor_reduce(neg_max[m % 2][:, j * T + s:j * T + s + 1], bank(4 + (ring_parity[0] + j) % 2),
                                              AX.X, ALU.max, negate=True).then_inc(ring_used, 1)
                        ring_parity[0] += G

                    def turn_maxima(ring, split, m):
                        eng.wait_ge(max_ring, ring + 1)
                        eng.wait_ge(max_split, split)
                        eng.tensor_copy(neg_max_T[m % 2][:], bank(4 + ring_parity[0] % 2)[0:G * T, 0:128]).then_inc(ring_used, 1)
                        ring_parity[0] += 1

                    def normalize(i, m):
                        p, g = m // NG, m % NG
                        sums = bank(6 + m % 2).rearrange("p (t j c) -> p t j c", t=T, j=G)
                        eng.wait_ge(att_T, i * GP + m + 1)
                        eng.reciprocal(recip[m % 2][:], sums[:, :, :, DK]).then_inc(recip_done, 1)
                        eng.wait_ge(recip_done, i * GP + m + 1)
                        if g == 0:
                            eng.wait_ge(x1_own, i * (2 * X1_OPS))
                        eng.tensor_tensor(att[p][:, :, g * G * DK:(g + 1) * G * DK].rearrange("p t (j d) -> p t j d", j=G),
                                          sums[:, :, :, 0:DK],
                                          recip[m % 2][:, :, :, None].to_broadcast([128, T, G, DK]), ALU.mult).then_inc(att_norm, 1)

                    def turn(i, last):
                        ring = i * (GP * RING) + 2 * G * T + 1
                        for m in range(GP):
                            for s in range(T):
                                if s == 1 and not (last and m == GP - 1):
                                    turn_maxima(ring, (i * GP + m) * 4, m + 1)
                                    ring = ring + 1
                                if not (last and m >= GP - 2):
                                    maxima(ring, m + 2, s)
                                    ring = ring + G
                                if s == 2 and m > 0:
                                    normalize(i, m - 1)
                        normalize(i, GP - 1)

                    for s in range(T):
                        maxima(G * s, 0, s)
                    for s in range(T):
                        maxima(G * (T + s), 1, s)
                    turn_maxima(2 * G * T, 0, 0)
                    with eng.Fori(0, B // 2 - 1) as i:
                        turn(i, False)
                    turn(B // 2 - 1, True)

                @block.gpsimd
                def _(eng):
                    def split(n, m, ring):
                        own = Chain(eng, max_split, n * 4, passed)
                        eng.wait_ge(ring_used, ring + 3)
                        eng.wait_ge(shift_loaded[m % 2], (n - m % 2) * 24)
                        eng.sem_inc(passed, 1)
                        split_in_three(own, neg_max_T[m % 2][:], max_rest[m % 2][:], max_parts[m % 2])

                    def add(i, p):
                        b = i * 2 + p
                        own = Chain(eng, x1_own, b * X1_OPS)
                        eng.wait_ge(att_norm, i * GP + (p + 1) * NG + 2)
                        for t in range(T):
                            ga = mod_row[:, bass.ds(b, 1), GA, :].rearrange("p a d -> p (a d)")
                            eng.tensor_tensor(gated[:, t, :], att[p][:, t, :], ga, ALU.mult).then_inc(x1_own, 1)
                        eng.wait_ge(x1_own, b * X1_OPS + T)
                        x1 = X[:, bass.ds(b * T, T), :]
                        eng.tensor_tensor(x1, x1, gated[:], ALU.add).then_inc(x1_own, 1)
                        eng.wait_ge(x1_own, (b + 1) * X1_OPS)

                    def turn(i, last):
                        ring = i * (GP * RING) + 2 * G * T + 1
                        for m in range(GP):
                            if not (last and m >= GP - 2):
                                ring = ring + G
                            if not (last and m == GP - 1):
                                split(i * GP + m + 1, m + 1, ring)
                                ring = ring + 1
                            if not (last and m >= GP - 2):
                                ring = ring + G * (T - 1)
                            if m == NG:
                                add(i, 0)
                        add(i, 1)

                    split(0, 0, 2 * G * T)
                    with eng.Fori(0, B // 2 - 1) as i:
                        turn(i, False)
                    turn(B // 2 - 1, True)

        H2 = sb("H2", [128, NT, D])
        logits = sb("logits", [128, NT, E])
        with ExitStack() as c3:
            def sb3(name, shape, dt=FP32):
                return c3.enter_context(nc.sbuf_tensor(name, shape, dt))

            stats = [sb3(f"r_stats{p}", [128, T, 6]) for p in (0, 1)]
            mean_var = [sb3(f"r_mean_var{p}", [128, T, 2]) for p in (0, 1)]
            rstd = [sb3(f"r_rstd{p}", [128, T]) for p in (0, 1)]
            xn = [sb3(f"r_xn{p}", [128, T, D]) for p in (0, 1)]
            hn = [sb3(f"r_hn{p}", [128, T, D]) for p in (0, 1)]
            hT = [sb3(f"r_hT{p}", [D, S]) for p in (0, 1)]
            ln2_own, std2_done, xn2_done, xn_used, h2_kept, h2T_done, h2T_out, logit_done, logit_out = (
                sem(n) for n in ("ln2_own", "std2_done", "xn2_done", "xn_used", "h2_kept", "h2T_done", "h2T_out", "logit_done", "logit_out"))
            with nc.Block() as block:
                @block.vector
                def _(eng):
                    def tile_of(b, t):
                        return X[:, bass.ds(b * T + t, 1), :].rearrange("p a d -> p (a d)")

                    def normalize(i, p):
                        b = i * 2 + p
                        eng.wait_ge(xn_used, i * (2 * 2))
                        for t in range(T):
                            eng.bn_stats(stats[p][:, t, :], tile_of(b, t)).then_inc(ln2_own, 1)
                        eng.wait_ge(ln2_own, b * LN_OPS + T)
                        eng.sem_inc(passed, 1)
                        for t in range(T):
                            eng.bn_aggr(mean_var[p][:, t, :], stats[p][:, t, :]).then_inc(ln2_own, 1)
                        eng.wait_ge(ln2_own, b * LN_OPS + 2 * T)
                        eng.tensor_copy(rstd[p][:], mean_var[p][:, :, 1]).then_inc(ln2_own, 1)
                        eng.wait_ge(std2_done, b + 1)
                        eng.reciprocal(rstd[p][:], rstd[p][:]).then_inc(ln2_own, 1)
                        eng.wait_ge(ln2_own, (b + 1) * LN_OPS)
                        for t in range(T):
                            eng.tensor_scalar(xn[p][:, t, :], tile_of(b, t), mean_var[p][:, t, 0:1], rstd[p][:, t:t + 1],
                                              ALU.subtract, ALU.mult).then_inc(xn2_done, 1)

                    def out_of_bank(i, p):
                        b = i * 2 + p
                        eng.wait_ge(logit_done, b + 1)
                        eng.tensor_copy(logits[:, bass.ds(b * T, T), :],
                                        bank(4 * p + 1)[:, 0:T * E].rearrange("p (t e) -> p t e", t=T)).then_inc(logit_out, 1)

                    with eng.Fori(0, B // 2) as i:
                        normalize(i, 0)
                        normalize(i, 1)
                        out_of_bank(i, 0)
                        out_of_bank(i, 1)

                @block.gpsimd
                def _(eng):
                    def batch(i, p):
                        b = i * 2 + p
                        cb = mod_row[:, bass.ds(b, 1), CB, :].to_broadcast([128, T, D])
                        sbias = mod_row[:, bass.ds(b, 1), SB, :].to_broadcast([128, T, D])
                        eng.wait_ge(xn2_done, (b + 1) * T)
                        eng.tensor_tensor(xn[p][:], xn[p][:], cb, ALU.mult).then_inc(xn_used, 1)
                        eng.wait_ge(xn_used, b * 2 + 1)
                        eng.wait_ge(h2T_done, i * 2)
                        eng.wait_ge(h2_kept, i * 2)
                        eng.tensor_tensor(hn[p][:], xn[p][:], sbias, ALU.add).then_inc(xn_used, 1)
                        eng.wait_ge(xn_used, b * 2 + 2)
                        eng.sem_inc(passed, 1)
                        eng.tensor_copy(H2[:, bass.ds(b * T, T), :], hn[p][:]).then_inc(h2_kept, 1)

                    with eng.Fori(0, B // 2) as i:
                        batch(i, 0)
                        batch(i, 1)

                @block.scalar
                def _(eng):
                    def root(i, p):
                        eng.wait_ge(ln2_own, (i * 2 + p) * LN_OPS + 2 * T + 1)
                        nc.scalar.activation(rstd[p][:], rstd[p][:], ACT.Sqrt, bias=eps[:]).then_inc(std2_done, 1)

                    def batch(i, p):
                        b = i * 2 + p
                        eng.wait_ge(h2T_done, b + 1)
                        eng.wait_ge(logit_done, i * 2)
                        nc.scalar.copy(hT[p][:], bank(4 * p)).then_inc(h2T_out, 1)

                    with eng.Fori(0, B // 2) as i:
                        root(i, 0)
                        root(i, 1)
                        batch(i, 0)
                        batch(i, 1)

                @block.tensor
                def _(eng):
                    def batch(i, p):
                        b = i * 2 + p
                        eng.wait_ge(xn_used, b * 2 + 2)
                        eng.wait_ge(h2T_out, i * 2)
                        for t in range(T):
                            ins = eng.transpose(bank(4 * p)[:, 128 * t:128 * (t + 1)], hn[p][:, t, :], ident)
                        ins.then_inc(h2T_done, 1)
                        eng.wait_ge(h2T_out, b + 1)
                        eng.wait_ge(logit_out, i * 2)
                        for t in range(T):
                            ins = eng.matmul(bank(4 * p + 1)[:, E * t:E * (t + 1)], hT[p][:, 128 * t:128 * (t + 1)], rw[:],
                                             start=True, stop=True)
                        ins.then_inc(logit_done, 1)

                    with eng.Fori(0, B // 2) as i:
                        batch(i, 0)
                        batch(i, 1)

        weight = sb("weight", [128, NT, 2])
        place = sb("place", [128, NT, 2], I32)
        tile_expert = sb("tile_expert", [1, NST], I32)
        with ExitStack() as c4:
            def sb4(name, shape, dt=FP32):
                return c4.enter_context(nc.sbuf_tensor(name, shape, dt))

            best = sb4("best", [128, 2, NT])
            hot = sb4("hot", [128, 2, NT, E])
            masked = sb4("masked", [128, NT, E])
            work = sb4("work", [128, NT, E])
            index = sb4("index", [128, NT])
            chosen = sb4("chosen", [128, NT, E])
            total = sb4("total", [128, NT, E])
            zeros = sb4("zeros", [128, NT])
            low = sb4("low", [128, NT, E])
            gap = sb4("gap", [128, NT])
            share = sb4("share", [128, NT])
            counts_i = sb4("counts_i", [128, E], I32)
            tiles = sb4("tiles", [128, E])
            tiles_to = sb4("tiles_to", [128, E])
            base = sb4("base", [128, E])
            beyond = sb4("beyond", [1, NST, E])
            expert_f = sb4("expert_f", [1, NST])
            place_f = sb4("place_f", [128, NT, 2])
            top_own, gap_done, share_done, ranks_done = (sem(n) for n in ("top_own", "gap_done", "share_done", "ranks_done"))

            def over_experts(a):
                return a[:, :, None].to_broadcast([128, NT, E])

            def over_tiles(a):
                return a[:, None, :].to_broadcast([128, NT, E])

            with nc.Block() as block:
                @block.vector
                def _(eng):
                    own = Chain(eng, top_own)
                    own.link(eng.memset(zeros[:], 0.0))
                    own.link(eng.memset(low[:], -3.0e38))
                    own.link(eng.tensor_copy(masked[:], logits[:]))
                    for n in range(2):
                        hot_n, best_n = hot[:, n, :, :], best[:, n, :]
                        own.link(eng.tensor_reduce(best_n, masked[:], AX.X, ALU.max))
                        own.link(eng.tensor_tensor(work[:], masked[:], over_experts(best_n), ALU.is_equal))
                        own.link(eng.tensor_tensor(work[:], work[:], over_tiles(to_end), ALU.mult))
                        own.link(eng.tensor_reduce(index[:], work[:], AX.X, ALU.min))
                        own.link(eng.tensor_tensor(hot_n, over_tiles(to_end), over_experts(index[:]), ALU.is_equal))
                        if n == 0:
                            own.link(eng.copy_predicated(masked[:], hot_n.bitcast(I32), low[:]))
                    eng.tensor_tensor(gap[:], best[:, 1, :], best[:, 0, :], ALU.subtract).then_inc(gap_done, 1)
                    own.link(eng.tensor_tensor(chosen[:], hot[:, 0, :, :], hot[:, 1, :, :], ALU.add))
                    eng.wait_ge(share_done, 1)
                    own.link(eng.tensor_scalar(gap[:], share[:], 1.0, None, ALU.add))
                    own.link(eng.reciprocal(weight[:, :, 0], gap[:]))
                    own.link(eng.tensor_tensor(weight[:, :, 1], weight[:, :, 0], share[:], ALU.mult))
                    eng.wait_ge(ranks_done, 2)
                    own.link(eng.tensor_copy(total[:], bank(1)[:, 0:NT * E].rearrange("p (n e) -> p n e", e=E)))
                    for e in range(E):
                        own.link(eng.tensor_tensor_scan(work[:, :, e], total[:, :, e], zeros[:], 0.0, ALU.add, ALU.add))
                    own.link(eng.tensor_scalar(counts_i[:], work[:, NT - 1, :], float(TS - 1), None, ALU.add))
                    own.link(eng.tensor_scalar(counts_i[:], counts_i[:], TS.bit_length() - 1, None, ALU.logical_shift_right))
                    own.link(eng.tensor_copy(tiles[:], counts_i[:]))
                    own.link(eng.tensor_tensor_scan(tiles_to[:], tiles[:], zeros[:, 0:E], 0.0, ALU.add, ALU.add))
                    own.link(eng.tensor_tensor(base[:], tiles_to[:], tiles[:], ALU.subtract))
                    own.link(eng.tensor_scalar(base[:], base[:], float(TS), None, ALU.mult))
                    own.link(eng.tensor_tensor(work[:], work[:], total[:], ALU.subtract))
                    own.link(eng.tensor_tensor(work[:], work[:], bank(0)[:, 0:NT * E].rearrange("p (n e) -> p n e", e=E), ALU.add))
                    own.link(eng.tensor_tensor(work[:], work[:], over_tiles(base[:]), ALU.add))
                    for n in range(2):
                        own.link(eng.tensor_tensor(masked[:], hot[:, n, :, :], work[:], ALU.mult))
                        own.link(eng.tensor_reduce(place_f[:, :, n], masked[:], AX.X, ALU.add))
                    own.link(eng.tensor_copy(place[:], place_f[:]))
                    own.link(eng.tensor_tensor(beyond[:], tile_number[0:1, :, None].to_broadcast([1, NST, E]),
                                               tiles_to[0:1, None, :].to_broadcast([1, NST, E]), ALU.is_ge))
                    own.link(eng.tensor_reduce(expert_f[:], beyond[:], AX.X, ALU.add))
                    own.link(eng.tensor_scalar(expert_f[:], expert_f[:], float(E - 1), None, ALU.min))
                    own.link(eng.tensor_copy(tile_expert[:], expert_f[:]))

                @block.scalar
                def _(eng):
                    eng.wait_ge(gap_done, 1)
                    nc.scalar.activation(share[:], gap[:], ACT.Exp, bias=zero[:]).then_inc(share_done, 1)

                @block.tensor
                def _(eng):
                    eng.wait_ge(top_own, 3 + 5 + 1 + 5 + 1)
                    flat = chosen[:].rearrange("p n e -> p (n e)")
                    eng.matmul(bank(0)[:, 0:NT * E], before, flat, start=True, stop=True).then_inc(ranks_done, 1)
                    eng.matmul(bank(1)[:, 0:NT * E], ones, flat, start=True, stop=True).then_inc(ranks_done, 1)

        row_s = [sb(f"row_s{p}", [128, D]) for p in (0, 1)]
        place_s = [sb(f"place_s{p}", [128, 2], I32) for p in (0, 1)]
        row_ready, row_sent = sem("row_ready"), [sem(f"row_sent{p}") for p in (0, 1)]
        with nc.Block() as block:
            @block.vector
            def _(eng):
                with eng.Fori(0, NT // 2) as i:
                    for p in (0, 1):
                        eng.wait_ge(row_sent[p], i * 32)
                        eng.tensor_copy(row_s[p][:], H2[:, bass.ds(i * 2 + p, 1), :].rearrange("p a d -> p (a d)")).then_inc(row_ready, 1)
                        eng.tensor_copy(place_s[p][:], place[:, bass.ds(i * 2 + p, 1), :].rearrange("p a d -> p (a d)")).then_inc(row_ready, 1)

            @block.gpsimd
            def _(eng):
                eng.wait_ge(experts_loaded, 5 * 16)
                with eng.Fori(0, NT // 2) as i:
                    for p in (0, 1):
                        eng.wait_ge(row_ready, (i * 2 + p) * 2 + 2)
                        eng.sem_inc(passed, 1)
                        for n in range(2):
                            eng.indirect_dma_start(x_sorted, bass.IndirectOffsetOnAxis(ap=place_s[p][:, n:n + 1], axis=0),
                                                   row_s[p][:], None).then_inc(row_sent[p], 16)
                for p in (0, 1):
                    eng.wait_ge(row_sent[p], NT // 2 * 32)

        with ExitStack() as c5:
            def sb5(name, shape, dt=FP32):
                return c5.enter_context(nc.sbuf_tensor(name, shape, dt))

            HALVES = TS // 128
            xs = [sb5(f"xs{p}", [128, HALVES, D]) for p in (0, 1)]
            xsT = [sb5(f"xsT{p}", [D, TS]) for p in (0, 1)]
            w1_now = [sb5(f"w1_now{p}", [128, F + FC]) for p in (0, 1)]
            hid = [sb5(f"hid{p}", [128, FC, TS]) for p in (0, 1)]
            ys = [sb5(f"ys{p}", [128, HALVES, D]) for p in (0, 1)]
            xs_loaded = [sem(f"xs_loaded{p}") for p in (0, 1)]
            ys_stored = [sem(f"ys_stored{p}") for p in (0, 1)]
            w_copied, xsT_done, xsT_out, up_done, gelu_done, down_done, y_out = (
                sem(n) for n in ("w_copied", "xsT_done", "xsT_out", "up_done", "gelu_done", "down_done", "y_out"))
            TURNS = (NST - 1) // 2

            def parity_turns(eng, tile):
                with eng.Fori(0, TURNS) as i:
                    tile(i, 0)
                    tile(i, 1)
                tile(TURNS, 0)

            def up_bank(p, c):
                return bank(2 * p + c // 2)[:, TS * (c % 2):TS * (c % 2 + 1)]

            with nc.Block() as block:
                @block.sync
                def _(eng):
                    def load(i, p):
                        eng.wait_ge(xsT_done, i * 2)
                        eng.dma_start(xs[p][:], x_sorted[bass.ds((i * 2 + p) * TS, TS), :].rearrange("(a q) d -> q a d", q=128)
                                      ).then_inc(xs_loaded[p], 16)

                    parity_turns(eng, load)

                @block.gpsimd
                def _(eng):
                    def store(i, p):
                        eng.wait_ge(y_out, i * 2 + p + 1)
                        eng.dma_start(y_sorted[bass.ds((i * 2 + p) * TS, TS), :].rearrange("(a q) d -> q a d", q=128), ys[p][:]
                                      ).then_inc(ys_stored[p], 16)

                    parity_turns(eng, store)
                    eng.wait_ge(ys_stored[0], (TURNS + 1) * 16)
                    eng.wait_ge(ys_stored[1], TURNS * 16)

                @block.vector
                def _(eng):
                    def first(i, p):
                        t = i * 2 + p
                        e = eng.value_load(tile_expert[0:1, bass.ds(t, 1)], min_val=0, max_val=E - 1)
                        eng.wait_ge(up_done, i * 2)
                        eng.wait_ge(gelu_done, i * (2 * FC))
                        eng.tensor_copy(w1_now[p][:], W1[:, bass.ds(e, 1), :].rearrange("p a f -> p (a f)")).then_inc(w_copied, 1)
                        eng.wait_ge(xsT_done, t + 1)
                        eng.tensor_copy(xsT[p][:], bank(4 + p)[:, 0:TS]).then_inc(xsT_out, 1)

                    def second(i, p):
                        t = i * 2 + p
                        e = eng.value_load(tile_expert[0:1, bass.ds(t, 1)], min_val=0, max_val=E - 1)
                        eng.wait_ge(down_done, t + 1)
                        eng.wait_ge(ys_stored[p], i * 16)
                        eng.tensor_tensor(ys[p][:], bank(6 + p)[:, 0:HALVES * D].rearrange("q (a d) -> q a d", a=HALVES),
                                          b2_row[:, bass.ds(e, 1), :].to_broadcast([128, HALVES, D]), ALU.add).then_inc(y_out, 1)

                    first(0, 0)
                    with eng.Fori(0, TURNS) as i:
                        first(i, 1)
                        second(i, 0)
                        first(i + 1, 0)
                        second(i, 1)
                    second(TURNS, 0)

                @block.scalar
                def _(eng):
                    def gelu(i, p):
                        t = i * 2 + p
                        eng.wait_ge(down_done, i * 2)
                        for c in range(FC):
                            eng.wait_ge(up_done, t * FC + (c | 1) + 1)
                            nc.scalar.activation(hid[p][:, c, :], up_bank(p, c), ACT.Gelu,
                                                 bias=w1_now[p][:, F + c:F + c + 1]).then_inc(gelu_done, 1)

                    parity_turns(eng, gelu)

                @block.tensor
                def _(eng):
                    def up(i, p):
                        t = i * 2 + p
                        eng.wait_ge(xs_loaded[p], (i + 1) * 16)
                        eng.wait_ge(xsT_out, i * 2)
                        for a in range(HALVES):
                            ins = eng.transpose(bank(4 + p)[:, 128 * a:128 * (a + 1)], xs[p][:, a, :], ident)
                        ins.then_inc(xsT_done, 1)
                        eng.wait_ge(w_copied, t + 1)
                        eng.wait_ge(xsT_out, t + 1)
                        eng.wait_ge(gelu_done, i * (2 * FC))
                        for c in range(FC):
                            eng.matmul(up_bank(p, c), w1_now[p][:, 128 * c:128 * (c + 1)], xsT[p][:], start=True, stop=True
                                       ).then_inc(up_done, 1)

                    def down(i, p):
                        t = i * 2 + p
                        e = eng.value_load(tile_expert[0:1, bass.ds(t, 1)], min_val=0, max_val=E - 1)
                        eng.wait_ge(gelu_done, (t + 1) * FC)
                        eng.wait_ge(y_out, i * 2)
                        for a in range(HALVES):
                            for c in range(FC):
                                ins = eng.matmul(bank(6 + p)[:, D * a:D * (a + 1)], hid[p][:, c, 128 * a:128 * (a + 1)],
                                                 W2[:, bass.ds(e, 1), c, :].rearrange("p a d -> p (a d)"),
                                                 start=(c == 0), stop=(c == FC - 1))
                        ins.then_inc(down_done, 1)

                    up(0, 0)
                    with eng.Fori(0, TURNS) as i:
                        up(i, 1)
                        down(i, 0)
                        up(i + 1, 0)
                        down(i, 1)
                    down(TURNS, 0)

        with ExitStack() as c6:
            def sb6(name, shape, dt=FP32):
                return c6.enter_context(nc.sbuf_tensor(name, shape, dt))

            place_g = [sb6(f"place_g{p}", [128, 2], I32) for p in (0, 1)]
            weight_g = [sb6(f"weight_g{p}", [128, 2]) for p in (0, 1)]
            y = [sb6(f"y{p}", [128, 2, D]) for p in (0, 1)]
            res = [sb6(f"res{p}", [128, D]) for p in (0, 1)]
            place_ready, mix_own = sem("place_ready"), sem("mix_own")
            y_loaded = [sem(f"y_loaded{p}") for p in (0, 1)]
            out_stored = [sem(f"out_stored{p}") for p in (0, 1)]
            MIX_OPS = 4
            with nc.Block() as block:
                @block.vector
                def _(eng):
                    def ready(i, p):
                        eng.wait_ge(y_loaded[p], i * 32)
                        eng.tensor_copy(place_g[p][:], place[:, bass.ds(i * 2 + p, 1), :].rearrange("p a d -> p (a d)")).then_inc(place_ready, 1)

                    def mix(i, p):
                        n = i * 2 + p
                        own = Chain(eng, mix_own, n * MIX_OPS)
                        w = weight[:, bass.ds(n, 1), :].rearrange("p a d -> p (a d)")
                        gb = mod_row[:, bass.ds(i // (T // 2), 1), GB, :].rearrange("p a d -> p (a d)")
                        eng.wait_ge(y_loaded[p], (i + 1) * 32)
                        eng.wait_ge(out_stored[p], i * 16)
                        own.link(eng.tensor_scalar(res[p][:], y[p][:, 0, :], w[:, 0:1], None, ALU.mult))
                        own.link(eng.scalar_tensor_tensor(res[p][:], y[p][:, 1, :], w[:, 1:2], res[p][:], ALU.mult, ALU.add))
                        own.link(eng.tensor_tensor(res[p][:], res[p][:], gb, ALU.mult))
                        own.link(eng.tensor_tensor(res[p][:], res[p][:], X[:, bass.ds(n, 1), :].rearrange("p a d -> p (a d)"), ALU.add))

                    ready(0, 0)
                    ready(0, 1)
                    with eng.Fori(0, NT // 2 - 1) as i:
                        mix(i, 0)
                        ready(i + 1, 0)
                        mix(i, 1)
                        ready(i + 1, 1)
                    mix(NT // 2 - 1, 0)
                    mix(NT // 2 - 1, 1)

                @block.gpsimd
                def _(eng):
                    with eng.Fori(0, NT // 2) as i:
                        for p in (0, 1):
                            eng.wait_ge(place_ready, i * 2 + p + 1)
                            eng.wait_ge(mix_own, i * (2 * MIX_OPS))
                            eng.sem_inc(passed, 1)
                            for n in range(2):
                                eng.indirect_dma_start(y[p][:, n, :], None, y_sorted,
                                                       bass.IndirectOffsetOnAxis(ap=place_g[p][:, n:n + 1], axis=0)).then_inc(y_loaded[p], 16)

                @block.sync
                def _(eng):
                    with eng.Fori(0, NT // 2) as i:
                        for p in (0, 1):
                            eng.wait_ge(mix_own, (i * 2 + p + 1) * MIX_OPS)
                            eng.dma_start(out_rows[bass.ds((i * 2 + p) * 128, 128), :], res[p][:]).then_inc(out_stored[p], 16)
                    for p in (0, 1):
                        eng.wait_ge(out_stored[p], NT // 2 * 16)


def kernel(L0_attn_x, L0_attn_Wq, L0_attn_Wk, L0_attn_Wv, L0_ffn_router_w, L0_ffn_w1, L0_ffn_b1, L0_ffn_w2, L0_ffn_b2,
           L0_c, L0_wmod):
    import ml_dtypes
    import numpy as np
    from concourse import bacc
    from concourse.bass_utils import run_bass_kernel_spmd

    def laid(a, *axes):
        a = np.asarray(a)
        return np.ascontiguousarray(a.transpose(axes) if axes else a)

    shift_rows = np.zeros((DK, S), ml_dtypes.bfloat16)
    shift_rows[0] = 1
    constants = np.zeros((128, 3 * 128 + E + NST), np.float32)
    constants[:, 0:128] = np.eye(128)
    constants[:, 128:256] = np.triu(np.ones((128, 128)), 1)
    constants[:, 256:384] = 1
    constants[:, 384:384 + E] = np.arange(-E, 0)
    constants[:, 384 + E:] = np.arange(NST)
    arrays = {
        "x": laid(L0_attn_x),
        "wq_t": laid(L0_attn_Wq, 1, 0),
        "wk_t": laid(L0_attn_Wk, 1, 0),
        "wv_t": laid(L0_attn_Wv, 1, 0),
        "router_t": laid(L0_ffn_router_w, 1, 0),
        "w1_t": laid(L0_ffn_w1, 2, 0, 1),
        "b1_t": laid(np.asarray(L0_ffn_b1).reshape(E, FC, 128), 2, 0, 1),
        "w2_t": laid(np.asarray(L0_ffn_w2).reshape(E, D, FC, 128), 3, 0, 2, 1),
        "b2": laid(L0_ffn_b2),
        "c_t": laid(L0_c, 1, 0),
        "wmod": laid(L0_wmod),
        "constants": constants,
        "shift_rows": shift_rows,
    }
    nc = bacc.Bacc("TRN2", target_bir_lowering=False, num_devices=1)
    args = [nc.dram_tensor(name, a.shape, mybir.dt.from_np(a.dtype), kind="ExternalInput").ap() for name, a in arrays.items()]
    out = nc.dram_tensor("out", (B, S, D), FP32, kind="ExternalOutput").ap()
    adaln_block(nc, *args, out)
    result = run_bass_kernel_spmd(nc, [arrays], core_ids=[0])
    return result.results[0]["out"]
```

```python
import concourse.bass as bass
from concourse import mybir
from contextlib import ExitStack

FP32 = mybir.dt.float32
BF16 = mybir.dt.bfloat16
I32 = mybir.dt.int32
ALU = mybir.AluOpType
ACT = mybir.ActivationFunctionType
AX = mybir.AxisListType

B, S, D = 8, 512, 128
NH, DK = 16, 8
T = S // 128
NT = B * T
E, F = 8, 512
FC = F // 128
TS = 256
NST = (2 * B * S + E * (TS - 1)) // TS
ROWS = NST * TS // 128
G = 4
NG = NH // G
SCALE = DK ** -0.5
EPS = 1e-5
QUAD = 32


CONSTS = 4 * 128 + E + NT + 3
START = 64

SEMAPHORES = """
    xn_done xT_done hT_done proj_done hi_done rest_done mid_done lo_done v_set v_copied max_ring ring_used max_T
    max_T_out score_done exp_done pv_done att_out att_T att_norm recip_done var2_done rstd2_own std2_done xn2_done
    xn_used h2T_done h2T_out logit_done logit_out top_own gap_done share_done ranks_done from_ready w_copied
    xsT_done xsT_out up_done gelu_done down_done y_out stored0 stored1 batch_loaded0 batch_loaded1 shift_loaded0
    shift_loaded1 h_stored0 h_stored1 y_loaded0 y_loaded1 c_loaded loaded experts_loaded passed dve_own silu_exp
    silu_done col_done col_out row_done row_out const_set op_set ones_loaded stat_own var_done std_done max_split
    x1_own guard_own marks_made marks_used first_done mix_own x_arrived0 x_arrived1 x_arrived2 x_arrived3
"""
FROM_ZERO = "gathered0 gathered1 scattered0 scattered1 out_stored0 out_stored1"


class Chain:

    def __init__(self, eng, sem, at=0, passed=None):
        self.eng, self.sem, self.at, self.passed = eng, sem, at, passed

    def link(self, ins):
        ins.then_inc(self.sem, 1)
        self.at = self.at + 1
        self.eng.wait_ge(self.sem, START + self.at)
        if self.passed:
            self.eng.sem_inc(self.passed, 1)


def split_in_three(own, whole, rest, part):
    own.link(own.eng.tensor_copy(part[0], whole))
    own.link(own.eng.tensor_tensor(rest, whole, part[0], ALU.subtract))
    own.link(own.eng.tensor_copy(part[1], rest))
    own.link(own.eng.tensor_tensor(part[2], rest, part[1], ALU.subtract))


def pipeline(eng, count, stages):
    most = max(ahead for _, ahead in stages)
    for t in range(-most, 0):
        for stage, ahead in stages:
            if 0 <= t + ahead < count:
                stage(t + ahead, (t + ahead) % 2)
    turns = (count - most) // 2
    with eng.Fori(0, turns) as i:
        for p in (0, 1):
            for stage, ahead in stages:
                stage(i * 2 + (p + ahead), (p + ahead) % 2)
    for t in range(2 * turns, count):
        for stage, ahead in stages:
            if t + ahead < count:
                stage(t + ahead, (t + ahead) % 2)


def adaln_block(nc, x, wq_t, wk_t, wv_t, router_t, w1_t, b1_t, w2_t, b2, c_t, wmod, constants, shift_rows, out):
    q_parts = nc.dram_tensor("q_parts", (B, 3, D, S), BF16, kind="Internal").ap()
    k_parts = nc.dram_tensor("k_parts", (B, 3 * DK, S), BF16, kind="Internal").ap()
    v_cols = nc.dram_tensor("v_cols", (B, 128, T * QUAD), FP32, kind="Internal").ap()

    h_rows = nc.dram_tensor("h_rows", (B * S, D), FP32, kind="Internal").ap()
    y_rows = nc.dram_tensor("y_rows", (2 * B * S + NST * TS, D), FP32, kind="Internal").ap()
    out_rows = out.rearrange("b s d -> (b s) d")

    ctx = ExitStack()
    with ctx:
        def sb(name, shape, dt=FP32):
            return ctx.enter_context(nc.sbuf_tensor(name, shape, dt))

        semaphores = {name: ctx.enter_context(nc.semaphore(name)) for name in (SEMAPHORES + FROM_ZERO).split()}
        sem = semaphores.get

        X = sb("X", [128, NT, D])
        consts = sb("consts", [128, CONSTS])
        ident, before, ones = (consts[:, 128 * n:128 * (n + 1)] for n in range(3))
        line = consts[:, 384:512]
        to_end, tile_number = consts[:, 512:512 + E], line[:, 0:NST]
        tile_after = consts[:, 512 + E:512 + E + NT]
        rest_of = consts[:, 512 + E + NT:512 + E + NT + 2]
        ident_b, line_b = sb("ident_b", [128, 128], BF16), sb("line_b", [128, 128], BF16)
        past_end = consts[:, CONSTS - 1:]
        wq = sb("wq", [D, D])
        wk = sb("wk", [D, DK])
        wv = sb("wv", [D, DK])
        rw = sb("rw", [D, E])
        wm = sb("wm", [D, 6 * D])
        W1 = sb("W1", [128, E, F + FC])
        W2 = sb("W2", [128, E, FC, D])
        b2_row = sb("b2_row", [128, E, D])
        cT = sb("cT", [D, B])
        siluT = sb("siluT", [D, B])
        silu_den = sb("silu_den", [D, B])
        silu_wide = sb("silu_wide", [D, B, 128])
        mod_col = sb("mod_col", [D, 2, B])
        mod_row = sb("mod_row", [128, B, 4, D])
        GA, SB, CB, GB = range(4)
        eps = sb("eps", [128, 1])
        zero = sb("zero", [128, 1])

        ps = ctx.enter_context(nc.psum_tensor("ps", [128, 8 * 512], FP32))

        def bank(n, count=1):
            return ps[:, 512 * n:512 * (n + count)]

        Q = [sb(f"Q{p}", [128, NH, S], BF16) for p in (0, 1)]
        KM = [sb(f"KM{p}", [128, S], BF16) for p in (0, 1)]
        KS = [sb(f"KS{p}", [128, S], BF16) for p in (0, 1)]
        ln_stats = sb("ln_stats", [128, NT, 6])

        XC = 4
        LOADED = 5 * 16
        c_loaded, loaded, experts_loaded = sem("c_loaded"), sem("loaded"), sem("experts_loaded")
        x_arrived = [sem(f"x_arrived{c}") for c in range(XC)]
        passed, dve_own, silu_exp, silu_done = sem("passed"), sem("dve_own"), sem("silu_exp"), sem("silu_done")
        col_done, col_out, row_done, row_out = sem("col_done"), sem("col_out"), sem("row_done"), sem("row_out")
        const_set, op_set, ones_loaded = sem("const_set"), sem("op_set"), sem("ones_loaded")
        stat_own, var_done, std_done = sem("stat_own"), sem("var_done"), sem("std_done")
        ROW_ORDER = list(range(1, B)) + [0]

        def one(tensor, n):
            return tensor[:, bass.ds(n, 1), :].rearrange("p a d -> p (a d)")

        def row_stats(eng, stats, b):
            for t in range(T):
                eng.bn_stats(one(stats, b * T + t), one(X, b * T + t)).then_inc(stat_own, 1)

        def variances(own, stats, mean, var, tmp):
            even, odd = stats[:, :, 1], stats[:, :, 4]
            own.link(own.eng.tensor_tensor(tmp[:], even, odd, ALU.subtract))
            own.link(own.eng.tensor_tensor(mean[:], even, odd, ALU.add))
            own.link(own.eng.tensor_scalar(mean[:], mean[:], 0.5, None, ALU.mult))
            own.link(own.eng.tensor_tensor(tmp[:], tmp[:], tmp[:], ALU.mult))
            own.link(own.eng.tensor_tensor(var[:], stats[:, :, 2], stats[:, :, 5], ALU.add))
            own.link(own.eng.tensor_scalar(var[:], var[:], 1.0 / D, None, ALU.mult))
            own.link(own.eng.scalar_tensor_tensor(var[:], tmp[:], 0.25, var[:], ALU.mult, ALU.add))

        with nc.Block() as block:
            def start(eng, k, of):
                for name in SEMAPHORES.split()[k::of]:
                    eng.sem_inc(sem(name), START)

            @block.sync
            def _(eng):
                eng.dma_start(cT[:], c_t).then_inc(c_loaded, 16)
                eng.dma_start(wm[:], wmod).then_inc(c_loaded, 16)
                eng.dma_start(consts[:], constants).then_inc(loaded, 16)
                eng.dma_start(wq[:], wq_t).then_inc(loaded, 16)
                eng.dma_start(wk[:], wk_t).then_inc(loaded, 16)
                eng.dma_start(wv[:], wv_t).then_inc(loaded, 16)
                eng.dma_start(rw[:], router_t).then_inc(loaded, 16)

            @block.scalar
            def _(eng):
                rows = x.rearrange("b (t p) d -> p (b t) d", p=128)
                for c, arrived in enumerate(x_arrived):
                    these = slice(c * NT // XC, (c + 1) * NT // XC)
                    eng.dma_start(X[:, these, :], rows[:, these, :]).then_inc(arrived, 16)

            @block.vector
            def _(eng):
                start(eng, 0, 3)

            @block.gpsimd
            def _(eng):
                start(eng, 1, 3)

            @block.tensor
            def _(eng):
                start(eng, 2, 3)

        ln_mean, ln_rstd, ln_tmp = (sb(n, [128, NT]) for n in ("ln_mean", "ln_rstd", "ln_tmp"))
        with nc.Block() as block:
            @block.sync
            def _(eng):
                eng.wait_ge(op_set, START + 2)
                for p in (0, 1):
                    for blk in range(3):
                        eng.dma_start(KS[p][QUAD * blk + 24:QUAD * blk + 32, :], shift_rows).then_inc(ones_loaded, 16)
                eng.wait_ge(x_arrived[-1], START + 16)
                eng.dma_start(W1[:, :, 0:F], w1_t).then_inc(experts_loaded, 16)
                eng.dma_start(W1[:, :, F:], b1_t).then_inc(experts_loaded, 16)
                eng.dma_start(W2[:], w2_t).then_inc(experts_loaded, 16)
                eng.dma_start(b2_row[:].rearrange("p e d -> p (e d)"), b2.rearrange("e d -> (e d)").partition_broadcast(128)).then_inc(experts_loaded, 16)

            @block.gpsimd
            def _(eng):
                for operand in (KS[0], KS[1], KM[0], KM[1], Q[0], Q[1]):
                    eng.memset(operand[:].bitcast(I32), 0).then_inc(op_set, 1)

            @block.scalar
            def _(eng):
                eng.wait_ge(c_loaded, START + 32)
                eng.wait_ge(const_set, START + 2)
                nc.scalar.activation(silu_den[:], cT[:], ACT.Exp, bias=zero[:], scale=-1.0).then_inc(silu_exp, 1)
                for n, b in enumerate(ROW_ORDER):
                    eng.wait_ge(row_done, START + n + 1)
                    nc.scalar.copy(mod_row[:, b, :, :].rearrange("p k d -> p (k d)"), bank(b)).then_inc(row_out, 1)
                eng.wait_ge(var_done, START + 7)
                nc.scalar.activation(ln_rstd[:], ln_rstd[:], ACT.Sqrt, bias=eps[:]).then_inc(std_done, 1)

            @block.vector
            def _(eng):
                own = Chain(eng, dve_own)
                eng.memset(eps[:], EPS).then_inc(const_set, 1)
                eng.memset(zero[:], 0.0).then_inc(const_set, 1)
                eng.wait_ge(silu_exp, START + 1)
                own.link(eng.tensor_scalar(silu_den[:], silu_den[:], 1.0, None, ALU.add))
                own.link(eng.reciprocal(silu_den[:], silu_den[:]))
                own.link(eng.tensor_tensor(siluT[:], silu_den[:], cT[:], ALU.mult))
                eng.tensor_copy(silu_wide[:], siluT[:, :, None].to_broadcast([D, B, 128])).then_inc(silu_done, 1)
                eng.wait_ge(loaded, START + LOADED)
                eng.tensor_copy(ident_b[:], ident).then_inc(dve_own, 1)
                eng.tensor_copy(line_b[:], line).then_inc(dve_own, 1)
                eng.wait_ge(col_done, START + 1)
                eng.tensor_copy(mod_col[:, 1, :], bank(0)[:, 0:B]).then_inc(col_out, 1)
                eng.tensor_scalar(mod_col[:, 0, :], bank(0)[:, B:2 * B], 1.0, None, ALU.add).then_inc(col_out, 1)
                for c, arrived in enumerate(x_arrived):
                    eng.wait_ge(arrived, START + 16)
                    for n in range(c * NT // XC, (c + 1) * NT // XC):
                        eng.bn_stats(ln_stats[:, n, :], X[:, n, :]).then_inc(stat_own, 1)
                eng.wait_ge(stat_own, START + NT)
                variances(Chain(eng, var_done), ln_stats, ln_mean, ln_rstd, ln_tmp)
                eng.wait_ge(std_done, START + 1)
                eng.reciprocal(ln_rstd[:], ln_rstd[:]).then_inc(var_done, 1)

            @block.tensor
            def _(eng):
                eng.wait_ge(c_loaded, START + 32)
                eng.wait_ge(silu_done, START + 1)
                eng.matmul(bank(0)[:, 0:B], wm[:, 0:D], siluT[:], start=True, stop=True)
                eng.matmul(bank(0)[:, B:2 * B], wm[:, D:2 * D], siluT[:], start=True, stop=True).then_inc(col_done, 1)
                for b in ROW_ORDER:
                    if b == 0:
                        eng.wait_ge(col_out, START + 2)
                    eng.matmul(bank(b), silu_wide[:, b, :], wm[:, 2 * D:6 * D], start=True, stop=True).then_inc(row_done, 1)

        with ExitStack() as c1:
            def sb1(name, shape, dt=FP32):
                return c1.enter_context(nc.sbuf_tensor(name, shape, dt))

            xn = [sb1(f"xn{p}", [128, T, D]) for p in (0, 1)]
            hT = [sb1(f"hT{p}", [D, S]) for p in (0, 1)]
            rest = [sb1(f"rest{p}", [D, 2, S]) for p in (0, 1)]
            parts = [sb1(f"parts{p}", [D, 2, 3, S], BF16) for p in (0, 1)]
            vcol = [sb1(f"vcol{p}", [128, T, QUAD]) for p in (0, 1)]
            xn_done, xT_done, hT_done, proj_done, hi_done, rest_done, mid_done, lo_done, v_set, v_copied = (
                sem(n) for n in ("xn_done", "xT_done", "hT_done", "proj_done", "hi_done", "rest_done", "mid_done", "lo_done", "v_set", "v_copied"))
            stored = [sem(f"stored{p}") for p in (0, 1)]

            def projected(p, n):
                return bank(4 * p + 1 + n)[0:(D, DK)[n], :]

            with nc.Block() as block:
                @block.vector
                def _(eng):
                    for p in (0, 1):
                        eng.memset(vcol[p][:], 0.0).then_inc(v_set, 1)
                    eng.wait_ge(v_set, START + 2)
                    for p in (0, 1):
                        eng.memset(vcol[p][:, :, DK:DK + 1], 1.0).then_inc(v_set, 1)
                    eng.wait_ge(v_set, START + 4)

                    def normalize(b, p):
                        eng.wait_ge(xT_done, START + b - 1)
                        for t in range(T):
                            eng.tensor_scalar(xn[p][:, t, :], one(X, b * T + t), ln_mean[:, bass.ds(b * T + t, 1)],
                                              ln_rstd[:, bass.ds(b * T + t, 1)], ALU.subtract, ALU.mult).then_inc(xn_done, 1)

                    def take(b, p):
                        eng.wait_ge(lo_done, START + (b - 1) * 2)
                        for n in (0, 1):
                            eng.wait_ge(hi_done, START + b * 2 + n + 1)
                            q = projected(p, n)
                            eng.tensor_tensor(rest[p][0:(D, DK)[n], n, :], q, parts[p][0:(D, DK)[n], n, 0, :], ALU.subtract).then_inc(rest_done, 1)
                        eng.wait_ge(stored[p], START + (b - p) * 24)
                        eng.tensor_copy(vcol[p][:, :, 0:DK],
                                        bank(4 * p + 3)[:, 0:T * DK].rearrange("p (t d) -> p t d", t=T)).then_inc(v_copied, 1)

                    pipeline(eng, B, [(normalize, 2), (take, 0)])

                @block.scalar
                def _(eng):
                    def modulate(b, p):
                        eng.wait_ge(xT_done, START + b + 1)
                        eng.wait_ge(proj_done, START + b - 1)
                        nc.scalar.activation(hT[p][:], bank(4 * p), ACT.Identity, bias=mod_col[:, 1, bass.ds(b, 1)],
                                             scale=mod_col[:, 0, bass.ds(b, 1)]).then_inc(hT_done, 1)

                    def hi(b, p):
                        eng.wait_ge(proj_done, START + b + 1)
                        eng.wait_ge(stored[p], START + (b - p) * 24)
                        for n in (0, 1):
                            nc.scalar.copy(parts[p][0:(D, DK)[n], n, 0, :], projected(p, n)).then_inc(hi_done, 1)

                    def mid(b, p):
                        for n in (0, 1):
                            eng.wait_ge(rest_done, START + b * 2 + n + 1)
                            nc.scalar.copy(parts[p][0:(D, DK)[n], n, 1, :], rest[p][0:(D, DK)[n], n, :]).then_inc(mid_done, 1)

                    pipeline(eng, B, [(mid, 0), (modulate, 2), (hi, 1)])

                @block.gpsimd
                def _(eng):
                    def lo(b, p):
                        for n in (0, 1):
                            eng.wait_ge(mid_done, START + b * 2 + n + 1)
                            eng.tensor_tensor(parts[p][0:(D, DK)[n], n, 2, :], rest[p][0:(D, DK)[n], n, :],
                                              parts[p][0:(D, DK)[n], n, 1, :], ALU.subtract).then_inc(lo_done, 1)

                    pipeline(eng, B, [(lo, 0)])

                @block.tensor
                def _(eng):
                    def turn_rows(b, p):
                        eng.wait_ge(xn_done, START + (b + 1) * T)
                        eng.wait_ge(hT_done, START + b - 1)
                        for t in range(T):
                            ins = eng.transpose(bank(4 * p)[:, 128 * t:128 * (t + 1)], xn[p][:, t, :], ident)
                        ins.then_inc(xT_done, 1)

                    def project(b, p):
                        eng.wait_ge(hT_done, START + b + 1)
                        eng.wait_ge(rest_done, START + (b - 1) * 2)
                        eng.wait_ge(v_copied, START + b - 1)
                        eng.matmul(projected(p, 0), wq[:], hT[p][:], start=True, stop=True)
                        eng.matmul(projected(p, 1), wk[:], hT[p][:], start=True, stop=True)
                        for t in range(T):
                            ins = eng.matmul(bank(4 * p + 3)[:, DK * t:DK * (t + 1)], hT[p][:, 128 * t:128 * (t + 1)], wv[:],
                                             start=True, stop=True)
                        ins.then_inc(proj_done, 1)

                    pipeline(eng, B, [(turn_rows, 1), (project, 0)])

                @block.sync
                def _(eng):
                    def store(b, p):
                        eng.wait_ge(v_copied, START + b + 1)
                        eng.dma_start(v_cols[bass.ds(b, 1), :, :].rearrange("a p c -> (a p) c"),
                                      vcol[p][:].rearrange("p t c -> p (t c)")).then_inc(stored[p], 16)
                        eng.wait_ge(lo_done, START + (b + 1) * 2)
                        eng.dma_start(q_parts[bass.ds(b, 1), :, :, :].rearrange("a i p t -> p (a i) t"),
                                      parts[p][:, 0, :, :]).then_inc(stored[p], 16)
                        eng.dma_start(k_parts[bass.ds(b, 1), :, :].rearrange("a (i p) t -> p (a i) t", p=DK),
                                      parts[p][0:DK, 1, :, :]).then_inc(stored[p], 16)

                    pipeline(eng, B, [(store, 0)])
                    eng.wait_ge(ones_loaded, START + 6 * 16)
                    for p in (0, 1):
                        eng.wait_ge(stored[p], START + B // 2 * 48)

        with ExitStack() as c2:
            def sb2(name, shape, dt=FP32):
                return c2.enter_context(nc.sbuf_tensor(name, shape, dt))

            V = [sb2(f"V{p}", [128, T, QUAD]) for p in (0, 1)]
            P = [sb2(f"P{p}", [128, G, S]) for p in (0, 1)]
            neg_max = [sb2(f"neg_max{p}", [128, G * T]) for p in (0, 1)]
            neg_max_T = [sb2(f"neg_max_T{p}", [G * T, 128]) for p in (0, 1)]
            max_rest = [sb2(f"max_rest{p}", [G * T, 128]) for p in (0, 1)]
            max_parts = [sb2(f"max_parts{p}", [G * T, 3, 128], BF16) for p in (0, 1)]
            att_u = [sb2(f"att_u{p}", [128, S]) for p in (0, 1)]
            recip = [sb2(f"recip{p}", [128, T, G]) for p in (0, 1)]
            att = [sb2(f"att{p}", [128, T, D]) for p in (0, 1)]
            gated = sb2("gated", [128, T, D])
            RING = G * T
            X1_OPS = T + 1
            GP = 2 * NG
            LOADS = 9 + 3 + 3 + 1
            max_ring, ring_used, max_T, max_T_out, score_done, exp_done, pv_done, att_out, att_T, att_norm, recip_done = (
                sem(n) for n in ("max_ring", "ring_used", "max_T", "max_T_out", "score_done", "exp_done", "pv_done", "att_out",
                                 "att_T", "att_norm", "recip_done"))
            max_split, x1_own, guard_own = sem("max_split"), sem("x1_own"), sem("guard_own")
            batch_loaded = [sem(f"batch_loaded{p}") for p in (0, 1)]
            shift_loaded = [sem(f"shift_loaded{p}") for p in (0, 1)]

            with nc.Block() as block:
                @block.sync
                def _(eng):
                    def load(b, p):
                        for blk in range(3):
                            for r in range(3):
                                at = QUAD * blk + DK * r
                                eng.dma_start(Q[p][at:at + DK, :, :],
                                              q_parts[bass.ds(b, 1), blk, :, :].rearrange("a (h d) t -> d (a h) t", d=DK)
                                              ).then_inc(batch_loaded[p], 16)
                            at = QUAD * blk
                            for K in (KM[p], KS[p]):
                                eng.dma_start(K[at:at + 3 * DK, :],
                                              k_parts[bass.ds(b, 1), :, :].rearrange("a p t -> (a p) t")).then_inc(batch_loaded[p], 16)
                        eng.dma_start(V[p][:].rearrange("p t c -> p (t c)"),
                                      v_cols[bass.ds(b, 1), :, :].rearrange("a p c -> (a p) c")).then_inc(batch_loaded[p], 16)

                    def shift(n_split, m):
                        p, h = (m // NG) % 2, (m % NG) * G
                        eng.wait_ge(max_split, START + n_split)
                        for blk in range(3):
                            at = QUAD * blk + 24
                            eng.dma_start(Q[p][at:at + 1, h:h + G, :], max_parts[m % 2][:, blk, :]).then_inc(shift_loaded[m % 2], 16)

                    def turn(i, last):
                        for m in range(GP):
                            if not (last and m == GP - 1):
                                shift((i * GP + m + 2) * 4, m + 1)
                            if m == NG and not last:
                                eng.wait_ge(pv_done, START + i * (GP * T) + NG * T)
                                load(i * 2 + 2, 0)
                            if m == GP - 1 and not last:
                                eng.wait_ge(pv_done, START + (i + 1) * (GP * T))
                                load(i * 2 + 3, 1)

                    load(0, 0)
                    load(1, 1)
                    shift(4, 0)
                    with eng.Fori(0, B // 2 - 1) as i:
                        turn(i, False)
                    turn(B // 2 - 1, True)

                @block.tensor
                def _(eng):
                    def maximum(unit, m, s, j):
                        eng.wait_ge(ring_used, START + unit - 1)
                        eng.matmul(bank(4 + j % 2), Q[(m // NG) % 2][:, (m % NG) * G + j, 128 * s:128 * (s + 1)],
                                   KM[(m // NG) % 2][:], start=True, stop=True).then_inc(max_ring, 1)

                    def turn_maxima(n, m):
                        eng.wait_ge(ring_used, START + (n + 1) * RING)
                        eng.wait_ge(exp_done, START + (n - 1) * (2 * T))
                        eng.transpose(bank(3)[0:G * T, 0:128], neg_max[m % 2][:], ident).then_inc(max_T, 1)

                    def scores(i, m, s, u, turned):
                        p = (m // NG) % 2
                        if s == 0 and u == 0:
                            eng.wait_ge(shift_loaded[m % 2], START + (i * (GP // 2) + m // 2 + 1) * 48)
                        eng.wait_ge(exp_done, START + i * (GP * T * 2) + (m * T + s) * 2 + u - 1)
                        if s == 0 and u == 1 and turned:
                            eng.wait_ge(max_T_out, START + i * GP + m + 2)
                        for j in range(2):
                            ins = eng.matmul(bank(2 * u + j), KS[p][:, 128 * s:128 * (s + 1)], Q[p][:, (m % NG) * G + 2 * u + j, :],
                                             start=True, stop=True)
                        ins.then_inc(score_done, 1)

                    def values(i, m, s, heads):
                        if heads[0] == 0:
                            eng.wait_ge(exp_done, START + i * (GP * T * 2) + (m * T + s) * 2 + 2)
                            if s == 0:
                                eng.wait_ge(att_norm, START + i * GP + m - 1)
                        for j in heads:
                            ins = eng.matmul(bank(6 + m % 2)[QUAD * j:QUAD * (j + 1), :], V[(m // NG) % 2][:, s, :], P[s % 2][:, j, :],
                                             start=(s == 0), stop=(s == T - 1), tile_position=(0, QUAD * j))
                        if heads[-1] == G - 1:
                            ins.then_inc(pv_done, 1)

                    def back(i, m):
                        eng.wait_ge(att_out, START + i * GP + m + 1)
                        for t in range(T):
                            ins = eng.transpose(bank(6 + m % 2)[:, 128 * t:128 * (t + 1)], att_u[m % 2][:, 128 * t:128 * (t + 1)],
                                                ident)
                        ins.then_inc(att_T, 1)

                    def values_before(i, m, s, heads):
                        if s > 0:
                            values(i, m, s - 1, heads)
                        elif m > 0:
                            values(i, m - 1, T - 1, heads)

                    def turn(i, last):
                        for m in range(GP):
                            for s in range(T):
                                ahead = not (last and m >= GP - 2)
                                if ahead and m == NG - 2 and s == 0:
                                    eng.wait_ge(batch_loaded[1], START + (i + 1) * (16 * LOADS))
                                if ahead and m == GP - 2 and s == 0:
                                    eng.wait_ge(batch_loaded[0], START + (i + 2) * (16 * LOADS))
                                for j in range(G):
                                    if ahead:
                                        maximum((i * GP + m + 2) * RING + s * G + j, m + 2, s, j)
                                    if j % 2 == 0:
                                        scores(i, m, s, j // 2, not (last and m == GP - 1))
                                    else:
                                        values_before(i, m, s, (j - 1, j))
                                    if s == 0 and j == 1 and not (last and m == GP - 1):
                                        turn_maxima(i * GP + m + 1, m + 1)
                                if s == 1 and m > 0:
                                    back(i, m - 1)
                        values(i, GP - 1, T - 1, range(G))
                        back(i, GP - 1)

                    eng.wait_ge(batch_loaded[0], START + 16 * LOADS)
                    for n in range(G * T):
                        maximum(n, 0, n // G, n % G)
                    turn_maxima(0, 0)
                    for n in range(G * T):
                        maximum(RING + n, 1, n // G, n % G)
                    with eng.Fori(0, B // 2 - 1) as i:
                        turn(i, False)
                    turn(B // 2 - 1, True)

                @block.scalar
                def _(eng):
                    def out_of_bank(i, m):
                        eng.wait_ge(pv_done, START + i * (GP * T) + (m + 1) * T)
                        nc.scalar.copy(att_u[m % 2][:], bank(6 + m % 2)).then_inc(att_out, 1)

                    def turn(i):
                        for m in range(GP):
                            for s in range(T):
                                eng.wait_ge(pv_done, START + i * (GP * T) + m * T + s - 1)
                                for u in range(2):
                                    eng.wait_ge(score_done, START + i * (GP * T * 2) + (m * T + s) * 2 + u + 1)
                                    nc.scalar.activation(P[s % 2][:, 2 * u:2 * u + 2, :],
                                                         bank(2 * u, 2).rearrange("p (j t) -> p j t", j=2),
                                                         ACT.Exp, bias=zero[:], scale=SCALE).then_inc(exp_done, 1)
                                if s == 0 and m > 0:
                                    out_of_bank(i, m - 1)
                        out_of_bank(i, GP - 1)

                    nc.scalar.preload_act_table(ACT.Exp)
                    with eng.Fori(0, B // 2) as i:
                        turn(i)

                @block.vector
                def _(eng):
                    def maxima(n, m, s, heads):
                        for j in heads:
                            eng.wait_ge(max_ring, START + n * RING + s * G + j + 1)
                            if s == 0 and j == 0:
                                eng.wait_ge(max_T, START + n - 1)
                            eng.tensor_reduce(neg_max[m % 2][:, j * T + s:j * T + s + 1], bank(4 + j % 2),
                                              AX.X, ALU.max, negate=True).then_inc(ring_used, 1)

                    def turn_maxima(n, m):
                        eng.wait_ge(max_T, START + n + 1)
                        eng.wait_ge(max_split, START + (n - 1) * 4)
                        eng.tensor_copy(neg_max_T[m % 2][:], bank(3)[0:G * T, 0:128]).then_inc(max_T_out, 1)

                    def normalize(i, m):
                        p, g = m // NG, m % NG
                        sums = bank(6 + m % 2).rearrange("p (t j c) -> p t j c", t=T, j=G)
                        eng.wait_ge(att_T, START + i * GP + m + 1)
                        eng.reciprocal(recip[m % 2][:], sums[:, :, :, DK]).then_inc(recip_done, 1)
                        eng.wait_ge(recip_done, START + i * GP + m + 1)
                        if g == 0:
                            eng.wait_ge(x1_own, START + (i * 2 + p - 1) * X1_OPS)
                        eng.tensor_tensor(att[p][:, :, g * G * DK:(g + 1) * G * DK].rearrange("p t (j d) -> p t j d", j=G),
                                          sums[:, :, :, 0:DK],
                                          recip[m % 2][:, :, :, None].to_broadcast([128, T, G, DK]), ALU.mult).then_inc(att_norm, 1)

                    def turn(i, last):
                        for m in range(GP):
                            for s in range(T):
                                ahead = not (last and m >= GP - 2)
                                if ahead:
                                    maxima(i * GP + m + 2, m + 2, s, (0, 1))
                                if s == 2 and m > 0:
                                    normalize(i, m - 1)
                                if s == 0 and not (last and m == GP - 1):
                                    turn_maxima(i * GP + m + 1, m + 1)
                                if ahead:
                                    maxima(i * GP + m + 2, m + 2, s, (2, 3))
                        normalize(i, GP - 1)

                    for s in range(T):
                        maxima(0, 0, s, range(G))
                    turn_maxima(0, 0)
                    for s in range(T):
                        maxima(1, 1, s, range(G))
                    with eng.Fori(0, B // 2 - 1) as i:
                        turn(i, False)
                    turn(B // 2 - 1, True)

                @block.gpsimd
                def _(eng):
                    def guard(g):
                        own = Chain(eng, guard_own, guarded[0])
                        own.link(eng.tensor_scalar(sign, g, 0.0, 2.0, ALU.is_ge, ALU.mult))
                        own.link(eng.tensor_scalar(sign, sign, -1.0, None, ALU.add))
                        own.link(eng.tensor_tensor(g, g, sign, ALU.mult))
                        own.link(eng.tensor_scalar(g, g, 0.25, None, ALU.max))
                        own.link(eng.tensor_tensor(g, g, sign, ALU.mult))
                        guarded[0] = own.at

                    def split(n, m):
                        p = m % 2
                        own = Chain(eng, max_split, n * 4, passed)
                        eng.wait_ge(max_T_out, START + n + 1)
                        eng.wait_ge(shift_loaded[p], START + (n - p) * 24)
                        eng.sem_inc(passed, 1)
                        split_in_three(own, neg_max_T[p][:], max_rest[p][:], [max_parts[p][:, part, :] for part in range(3)])

                    def add(i, p):
                        b = i * 2 + p
                        own = Chain(eng, x1_own, b * X1_OPS)
                        eng.wait_ge(att_norm, START + i * GP + (p + 1) * NG)
                        for t in range(T):
                            ga = mod_row[:, bass.ds(b, 1), GA, :].rearrange("p a d -> p (a d)")
                            eng.tensor_tensor(gated[:, t, :], att[p][:, t, :], ga, ALU.mult).then_inc(x1_own, 1)
                        eng.wait_ge(x1_own, START + b * X1_OPS + T)
                        x1 = X[:, bass.ds(b * T, T), :]
                        eng.tensor_tensor(x1, x1, gated[:], ALU.add).then_inc(x1_own, 1)
                        eng.wait_ge(x1_own, START + (b + 1) * X1_OPS)

                    def turn(i, last):
                        for m in range(GP):
                            if not (last and m == GP - 1):
                                split(i * GP + m + 1, m + 1)
                            if m == NG:
                                add(i, 0)
                        add(i, 1)

                    guarded, sign = [0], gated[:, 0:4, :]
                    for kind in (GA, GB):
                        for half in range(0, B, 4):
                            guard(mod_row[:, half:half + 4, kind, :])
                    cb = mod_row[:, :, CB, :]
                    Chain(eng, guard_own, guarded[0]).link(eng.tensor_scalar(cb, cb, 1.0, None, ALU.add))
                    split(0, 0)
                    with eng.Fori(0, B // 2 - 1) as i:
                        turn(i, False)
                    turn(B // 2 - 1, True)

        logits = sb("logits", [128, NT, E])
        with ExitStack() as c3:
            def sb3(name, shape, dt=FP32):
                return c3.enter_context(nc.sbuf_tensor(name, shape, dt))

            stats = sb3("r_stats", [128, NT, 6])
            mean, rstd, tmp = (sb3(n, [128, NT]) for n in ("r_mean", "r_rstd", "r_tmp"))
            xn = [sb3(f"r_xn{p}", [128, T, D]) for p in (0, 1)]
            hn = [sb3(f"r_hn{p}", [128, T, D]) for p in (0, 1)]
            hT = [sb3(f"r_hT{p}", [D, S]) for p in (0, 1)]
            var2_done, rstd2_own, std2_done, xn2_done, xn_used, h2T_done, h2T_out, logit_done, logit_out = (
                sem(n) for n in ("var2_done", "rstd2_own", "std2_done", "xn2_done", "xn_used", "h2T_done", "h2T_out", "logit_done", "logit_out"))
            h_stored = [sem(f"h_stored{p}") for p in (0, 1)]
            with nc.Block() as block:
                @block.vector
                def _(eng):
                    with eng.Fori(0, B) as b:
                        row_stats(eng, stats, b)
                    eng.wait_ge(stat_own, START + 2 * NT)
                    variances(Chain(eng, var2_done), stats, mean, rstd, tmp)
                    eng.wait_ge(std2_done, START + 1)
                    eng.reciprocal(rstd[:], rstd[:]).then_inc(rstd2_own, 1)
                    eng.wait_ge(rstd2_own, START + 1)

                    def normalize(b, p):
                        eng.wait_ge(xn_used, START + b - 1)
                        for t in range(T):
                            eng.tensor_scalar(xn[p][:, t, :], one(X, b * T + t), mean[:, bass.ds(b * T + t, 1)],
                                              rstd[:, bass.ds(b * T + t, 1)], ALU.subtract, ALU.mult).then_inc(xn2_done, 1)
                        eng.wait_ge(xn2_done, START + b * (T + 1) + T)
                        cb = mod_row[:, bass.ds(b, 1), CB, :].to_broadcast([128, T, D])
                        eng.tensor_tensor(xn[p][:], xn[p][:], cb, ALU.mult).then_inc(xn2_done, 1)

                    def out_of_bank(b, p):
                        eng.wait_ge(logit_done, START + b + 1)
                        eng.tensor_copy(logits[:, bass.ds(b * T, T), :],
                                        bank(4 * p + 1)[:, 0:T * E].rearrange("p (t e) -> p t e", t=T)).then_inc(logit_out, 1)

                    pipeline(eng, B, [(normalize, 2), (out_of_bank, 0)])

                @block.gpsimd
                def _(eng):
                    def batch(b, p):
                        sbias = mod_row[:, bass.ds(b, 1), SB, :].to_broadcast([128, T, D])
                        eng.wait_ge(xn2_done, START + (b + 1) * (T + 1))
                        eng.wait_ge(h2T_done, START + b - 1)
                        eng.wait_ge(h_stored[p], START + (b - p) * 8)
                        eng.tensor_tensor(hn[p][:], xn[p][:], sbias, ALU.add).then_inc(xn_used, 1)

                    pipeline(eng, B, [(batch, 0)])

                @block.sync
                def _(eng):
                    def batch(b, p):
                        eng.wait_ge(xn_used, START + b + 1)
                        eng.dma_start(h_rows[bass.ds(b * S, S), :].rearrange("(t p) d -> p t d", p=128), hn[p][:]).then_inc(h_stored[p], 16)

                    pipeline(eng, B, [(batch, 0)])
                    for p in (0, 1):
                        eng.wait_ge(h_stored[p], START + B // 2 * 16)

                @block.scalar
                def _(eng):
                    def batch(b, p):
                        eng.wait_ge(h2T_done, START + b + 1)
                        eng.wait_ge(logit_done, START + b - 1)
                        nc.scalar.copy(hT[p][:], bank(4 * p)).then_inc(h2T_out, 1)

                    eng.wait_ge(var2_done, START + 7)
                    nc.scalar.activation(rstd[:], rstd[:], ACT.Sqrt, bias=eps[:]).then_inc(std2_done, 1)
                    pipeline(eng, B, [(batch, 0)])

                @block.tensor
                def _(eng):
                    def turn_rows(b, p):
                        eng.wait_ge(xn_used, START + b + 1)
                        eng.wait_ge(h2T_out, START + b - 1)
                        for t in range(T):
                            ins = eng.transpose(bank(4 * p)[:, 128 * t:128 * (t + 1)], hn[p][:, t, :], ident)
                        ins.then_inc(h2T_done, 1)

                    def route(b, p):
                        eng.wait_ge(h2T_out, START + b + 1)
                        eng.wait_ge(logit_out, START + b - 1)
                        for t in range(T):
                            ins = eng.matmul(bank(4 * p + 1)[:, E * t:E * (t + 1)], hT[p][:, 128 * t:128 * (t + 1)], rw[:],
                                             start=True, stop=True)
                        ins.then_inc(logit_done, 1)

                    pipeline(eng, B, [(turn_rows, 1), (route, 0)])

        weight = sb("weight", [128, NT, 2])
        from_row = sb("from_row", [128, ROWS], I32)
        to_row = sb("to_row", [128, ROWS], I32)
        tile_expert = sb("tile_expert", [1, NST], I32)
        with ExitStack() as c4:
            def sb4(name, shape, dt=FP32):
                return c4.enter_context(nc.sbuf_tensor(name, shape, dt))

            best = sb4("best", [128, 2, NT])
            hot = sb4("hot", [128, 2, NT, E])
            masked = sb4("masked", [128, NT, E])
            work = sb4("work", [128, NT, E])
            index = sb4("index", [128, NT])
            chosen = sb4("chosen", [128, NT, E])
            total = sb4("total", [128, NT, E])
            zeros = sb4("zeros", [128, NT])
            low = sb4("low", [128, NT, E])
            gap = sb4("gap", [128, NT])
            share = sb4("share", [128, NT])
            counts_i = sb4("counts_i", [128, E], I32)
            tiles = sb4("tiles", [128, E])
            tiles_to = sb4("tiles_to", [128, E])
            base = sb4("base", [128, E])
            beyond = sb4("beyond", [1, NST, E])
            expert_f = sb4("expert_f", [1, NST])
            place = sb4("place", [128, NT, 2])
            place_i = sb4("place_i", [128, NT, 2], I32)
            high = sb4("high", [128, NT, 2])
            is_low = [[sb4(f"is_low{p}{n}", [128, 128], BF16) for n in (0, 1)] for p in (0, 1)]
            by_high = [[sb4(f"by_high{p}{n}", [128, 2, ROWS], BF16) for n in (0, 1)] for p in (0, 1)]
            found, found_rest = sb4("found", [128, ROWS]), sb4("found_rest", [128, ROWS])
            empty = sb4("empty", [128, ROWS])
            beside = sb4("beside", [128, ROWS])
            marks_made, marks_used = sem("marks_made"), sem("marks_used")
            top_own, gap_done, share_done, ranks_done = (sem(n) for n in ("top_own", "gap_done", "share_done", "ranks_done"))

            def over_experts(a):
                return a[:, :, None].to_broadcast([128, NT, E])

            def over_tiles(a):
                return a[:, None, :].to_broadcast([128, NT, E])

            with nc.Block() as block:
                @block.vector
                def _(eng):
                    own = Chain(eng, top_own)
                    own.link(eng.memset(zeros[:], 0.0))
                    own.link(eng.memset(low[:], -3.0e38))
                    own.link(eng.tensor_copy(masked[:], logits[:]))
                    for n in range(2):
                        hot_n, best_n = hot[:, n, :, :], best[:, n, :]
                        own.link(eng.tensor_reduce(best_n, masked[:], AX.X, ALU.max))
                        own.link(eng.tensor_tensor(work[:], masked[:], over_experts(best_n), ALU.is_equal))
                        own.link(eng.tensor_tensor(work[:], work[:], over_tiles(to_end), ALU.mult))
                        own.link(eng.tensor_reduce(index[:], work[:], AX.X, ALU.min))
                        own.link(eng.tensor_tensor(hot_n, over_tiles(to_end), over_experts(index[:]), ALU.is_equal))
                        if n == 0:
                            own.link(eng.copy_predicated(masked[:], hot_n.bitcast(I32), low[:]))
                    eng.tensor_tensor(gap[:], best[:, 1, :], best[:, 0, :], ALU.subtract).then_inc(gap_done, 1)
                    own.link(eng.tensor_tensor(chosen[:], hot[:, 0, :, :], hot[:, 1, :, :], ALU.add))
                    eng.wait_ge(share_done, START + 1)
                    own.link(eng.tensor_scalar(gap[:], share[:], 1.0, None, ALU.add))
                    own.link(eng.reciprocal(weight[:, :, 0], gap[:]))
                    own.link(eng.tensor_tensor(weight[:, :, 1], weight[:, :, 0], share[:], ALU.mult))
                    eng.wait_ge(ranks_done, START + 2)
                    own.link(eng.tensor_copy(total[:], bank(1)[:, 0:NT * E].rearrange("p (n e) -> p n e", e=E)))
                    for e in range(E):
                        own.link(eng.tensor_tensor_scan(work[:, :, e], total[:, :, e], zeros[:], 0.0, ALU.add, ALU.add))
                    own.link(eng.tensor_scalar(counts_i[:], work[:, NT - 1, :], float(TS - 1), None, ALU.add))
                    own.link(eng.tensor_scalar(counts_i[:], counts_i[:], TS.bit_length() - 1, None, ALU.logical_shift_right))
                    own.link(eng.tensor_copy(tiles[:], counts_i[:]))
                    own.link(eng.tensor_tensor_scan(tiles_to[:], tiles[:], zeros[:, 0:E], 0.0, ALU.add, ALU.add))
                    own.link(eng.tensor_tensor(base[:], tiles_to[:], tiles[:], ALU.subtract))
                    own.link(eng.tensor_scalar(base[:], base[:], float(TS), None, ALU.mult))
                    own.link(eng.tensor_tensor(work[:], work[:], total[:], ALU.subtract))
                    own.link(eng.tensor_tensor(work[:], work[:], bank(0)[:, 0:NT * E].rearrange("p (n e) -> p n e", e=E), ALU.add))
                    own.link(eng.tensor_tensor(work[:], work[:], over_tiles(base[:]), ALU.add))
                    for n in range(2):
                        own.link(eng.tensor_tensor(masked[:], hot[:, n, :, :], work[:], ALU.mult))
                        own.link(eng.tensor_reduce(place[:, :, n], masked[:], AX.X, ALU.add))
                    own.link(eng.tensor_copy(place_i[:], place[:]))
                    own.link(eng.tensor_scalar(place_i[:], place_i[:], 7, None, ALU.logical_shift_right))
                    own.link(eng.tensor_copy(high[:], place_i[:]))
                    own.link(eng.scalar_tensor_tensor(place[:], high[:], -128.0, place[:], ALU.mult, ALU.add))

                    def marks(t, p):
                        eng.wait_ge(marks_used, START + (t - 1) * 2)
                        for n in range(2):
                            lo, hi = one(place, t)[:, n:n + 1], one(high, t)[:, n:n + 1]
                            eng.tensor_scalar(is_low[p][n][:], line_b[:, 0:128], lo, None, ALU.is_equal).then_inc(marks_made, 1)
                            eng.tensor_scalar(by_high[p][n][:, 0, :], line_b[:, 0:ROWS], hi, tile_after[:, bass.ds(t, 1)],
                                              ALU.is_equal, ALU.mult).then_inc(marks_made, 1)
                            eng.tensor_scalar(by_high[p][n][:, 1, :], line_b[:, 0:ROWS], hi, rest_of[:, n:n + 1],
                                              ALU.is_equal, ALU.mult).then_inc(marks_made, 1)

                    pipeline(eng, NT, [(marks, 0)])
                    eng.wait_ge(marks_used, START + NT * 2)
                    sums = bank(2)[:, 0:2 * ROWS].rearrange("p (a k) -> p a k", a=2)
                    own.link(eng.tensor_copy(found_rest[:], sums[:, 1, :]))
                    own.link(eng.scalar_tensor_tensor(found[:], sums[:, 0, :], 2.0 * 128, found_rest[:], ALU.mult, ALU.add))
                    own.link(eng.tensor_scalar(found[:], found[:], 1.0 - 2 * 128, 0.0, ALU.add, ALU.max))
                    own.link(eng.tensor_scalar(empty[:], found[:], 0.0, None, ALU.is_equal))
                    own.link(eng.tensor_scalar(beside[:], line[:, 0:ROWS], 128.0, past_end, ALU.mult, ALU.add))
                    own.link(eng.tensor_tensor(empty[:], empty[:], beside[:], ALU.mult))
                    own.link(eng.scalar_tensor_tensor(to_row[:], found[:], -1.0, empty[:], ALU.add, ALU.add))
                    own.link(eng.tensor_scalar(from_row[:], found[:], 1.0, -1.0, ALU.max, ALU.add))
                    own.link(eng.tensor_scalar(from_row[:], from_row[:], 1, None, ALU.logical_shift_right))
                    own.link(eng.tensor_tensor(beyond[:], tile_number[0:1, :, None].to_broadcast([1, NST, E]),
                                               tiles_to[0:1, None, :].to_broadcast([1, NST, E]), ALU.is_ge))
                    own.link(eng.tensor_reduce(expert_f[:], beyond[:], AX.X, ALU.add))
                    own.link(eng.tensor_scalar(expert_f[:], expert_f[:], float(E - 1), None, ALU.min))
                    own.link(eng.tensor_copy(tile_expert[:], expert_f[:]))

                @block.scalar
                def _(eng):
                    eng.wait_ge(gap_done, START + 1)
                    nc.scalar.activation(share[:], gap[:], ACT.Exp, bias=zero[:]).then_inc(share_done, 1)

                @block.tensor
                def _(eng):
                    eng.wait_ge(top_own, START + 3 + 5 + 1 + 5 + 1)
                    flat = chosen[:].rearrange("p n e -> p (n e)")
                    eng.matmul(bank(0)[:, 0:NT * E], before, flat, start=True, stop=True).then_inc(ranks_done, 1)
                    eng.matmul(bank(1)[:, 0:NT * E], ones, flat, start=True, stop=True).then_inc(ranks_done, 1)

                    def add_marks(t, p, first=False, final=False):
                        for n in range(2):
                            eng.wait_ge(marks_made, START + t * 6 + 3 * n + 3)
                            eng.matmul(bank(2)[:, 0:2 * ROWS], is_low[p][n][:], by_high[p][n][:].rearrange("p a k -> p (a k)"),
                                       start=first and n == 0, stop=final and n == 1).then_inc(marks_used, 1)

                    add_marks(0, 0, first=True)
                    add_marks(1, 1)
                    with eng.Fori(1, NT // 2 - 1) as i:
                        add_marks(i * 2, 0)
                        add_marks(i * 2 + 1, 1)
                    add_marks(NT - 2, 0)
                    add_marks(NT - 1, 1, final=True)

        with ExitStack() as c5:
            def sb5(name, shape, dt=FP32):
                return c5.enter_context(nc.sbuf_tensor(name, shape, dt))

            HALVES = TS // 128
            xs = [sb5(f"xs{p}", [128, HALVES, D]) for p in (0, 1)]
            xsT = [sb5(f"xsT{p}", [D, TS]) for p in (0, 1)]
            from_now = [sb5(f"from_now{p}", [128, HALVES], I32) for p in (0, 1)]
            to_now = [sb5(f"to_now{p}", [128, HALVES], I32) for p in (0, 1)]
            w1_now = [sb5(f"w1_now{p}", [128, F + FC]) for p in (0, 1)]
            hid = [sb5(f"hid{p}", [128, FC, TS]) for p in (0, 1)]
            ys = [sb5(f"ys{p}", [128, HALVES, D]) for p in (0, 1)]
            gathered = [sem(f"gathered{p}") for p in (0, 1)]
            scattered = [sem(f"scattered{p}") for p in (0, 1)]
            from_ready, w_copied, xsT_done, xsT_out, up_done, gelu_done, down_done, y_out = (
                sem(n) for n in ("from_ready", "w_copied", "xsT_done", "xsT_out", "up_done", "gelu_done", "down_done", "y_out"))

            def expert_of(eng, t):
                return eng.value_load(tile_expert[0:1, bass.ds(t, 1)], min_val=0, max_val=E - 1)

            def up_bank(p, c):
                return bank(2 * p + c // 2)[:, TS * (c % 2):TS * (c % 2 + 1)]

            with nc.Block() as block:
                @block.gpsimd
                def _(eng):
                    def gather(t, p):
                        eng.wait_ge(from_ready, START + t + 1)
                        eng.wait_ge(xsT_done, START + t - 1)
                        eng.sem_inc(passed, 1)
                        for a in range(HALVES):
                            eng.indirect_dma_start(xs[p][:, a, :], None, h_rows,
                                                   bass.IndirectOffsetOnAxis(ap=from_now[p][:, a:a + 1], axis=0)).then_inc(gathered[p], 16)

                    def scatter(t, p):
                        eng.wait_ge(y_out, START + (t + 1) * 2)
                        eng.sem_inc(passed, 1)
                        for a in range(HALVES):
                            eng.indirect_dma_start(y_rows, bass.IndirectOffsetOnAxis(ap=to_now[p][:, a:a + 1], axis=0),
                                                   ys[p][:, a, :], None).then_inc(scattered[p], 16)

                    pipeline(eng, NST, [(scatter, 0), (gather, 4)])
                    eng.wait_ge(scattered[0], (NST + 1) // 2 * (16 * HALVES))
                    eng.wait_ge(scattered[1], NST // 2 * (16 * HALVES))

                @block.vector
                def _(eng):
                    def where_from(t, p):
                        eng.wait_ge(xsT_done, START + t - 1)
                        eng.tensor_copy(from_now[p][:], from_row[:, bass.ds(t * HALVES, HALVES)]).then_inc(from_ready, 1)

                    def weights(t, p):
                        e = expert_of(eng, t)
                        eng.wait_ge(up_done, START + (t - 1) * 2)
                        eng.wait_ge(gelu_done, START + (t - 1) * FC)
                        eng.tensor_copy(w1_now[p][:], one(W1, e)).then_inc(w_copied, 1)

                    def transposed(t, p):
                        eng.wait_ge(xsT_done, START + t + 1)
                        eng.wait_ge(up_done, START + (t - 1) * 2)
                        eng.tensor_copy(xsT[p][:], bank(4 + p)[:, 0:TS]).then_inc(xsT_out, 1)

                    def results(t, p):
                        e = expert_of(eng, t)
                        eng.wait_ge(scattered[p], (t - p) * (8 * HALVES))
                        eng.tensor_copy(to_now[p][:], to_row[:, bass.ds(t * HALVES, HALVES)]).then_inc(y_out, 1)
                        eng.wait_ge(down_done, START + t + 1)
                        eng.tensor_tensor(ys[p][:], bank(6 + p)[:, 0:HALVES * D].rearrange("q (a d) -> q a d", a=HALVES),
                                          b2_row[:, bass.ds(e, 1), :].to_broadcast([128, HALVES, D]), ALU.add).then_inc(y_out, 1)

                    pipeline(eng, NST, [(where_from, 4), (transposed, 2), (weights, 1), (results, 0)])

                @block.scalar
                def _(eng):
                    def gelu(t, p):
                        eng.wait_ge(down_done, START + t - 1)
                        for c in range(FC):
                            eng.wait_ge(up_done, START + t * 2 + c // 2 + 1)
                            nc.scalar.activation(hid[p][:, c, :], up_bank(p, c), ACT.Gelu,
                                                 bias=w1_now[p][:, F + c:F + c + 1]).then_inc(gelu_done, 1)

                    nc.scalar.preload_act_table(ACT.Gelu)
                    pipeline(eng, NST, [(gelu, 0)])

                @block.tensor
                def _(eng):
                    def turn_rows(t, p):
                        eng.wait_ge(gathered[p], (t - p + 2) * (8 * HALVES))
                        eng.wait_ge(xsT_out, START + t - 1)
                        for a in range(HALVES):
                            ins = eng.transpose(bank(4 + p)[:, 128 * a:128 * (a + 1)], xs[p][:, a, :], ident)
                        ins.then_inc(xsT_done, 1)

                    def up(t, p):
                        eng.wait_ge(w_copied, START + t + 1)
                        eng.wait_ge(xsT_out, START + t + 1)
                        eng.wait_ge(gelu_done, START + (t - 1) * FC)
                        for c in range(FC):
                            ins = eng.matmul(up_bank(p, c), w1_now[p][:, 128 * c:128 * (c + 1)], xsT[p][:], start=True, stop=True)
                            if c % 2:
                                ins.then_inc(up_done, 1)

                    def down(t, p):
                        e = expert_of(eng, t)
                        eng.wait_ge(gelu_done, START + (t + 1) * FC)
                        eng.wait_ge(y_out, START + (t - 1) * 2)
                        for a in range(HALVES):
                            for c in range(FC):
                                ins = eng.matmul(bank(6 + p)[:, D * a:D * (a + 1)], hid[p][:, c, 128 * a:128 * (a + 1)],
                                                 W2[:, bass.ds(e, 1), c, :].rearrange("p a d -> p (a d)"),
                                                 start=(c == 0), stop=(c == FC - 1))
                        ins.then_inc(down_done, 1)

                    pipeline(eng, NST, [(turn_rows, 2), (up, 1), (down, 0)])

        with ExitStack() as c6:
            def sb6(name, shape, dt=FP32):
                return c6.enter_context(nc.sbuf_tensor(name, shape, dt))

            y = [sb6(f"y{p}", [128, T, 2, D]) for p in (0, 1)]
            first = [sb6(f"first{p}", [128, T, D]) for p in (0, 1)]
            res = [sb6(f"res{p}", [128, T, D]) for p in (0, 1)]
            first_done, mix_own = sem("first_done"), sem("mix_own")
            y_loaded = [sem(f"y_loaded{p}") for p in (0, 1)]
            out_stored = [sem(f"out_stored{p}") for p in (0, 1)]
            MIX_OPS = T + 2
            with nc.Block() as block:
                @block.sync
                def _(eng):
                    def load(b, p):
                        eng.wait_ge(mix_own, START + (b - 1) * MIX_OPS)
                        eng.dma_start(y[p][:], y_rows[bass.ds(b * (2 * S), 2 * S), :].rearrange("(t p n) d -> p t n d", p=128, n=2)
                                      ).then_inc(y_loaded[p], 16)

                    pipeline(eng, B, [(load, 0)])

                @block.scalar
                def _(eng):
                    def batch(b, p):
                        eng.wait_ge(y_loaded[p], START + (b - p + 2) * 8)
                        eng.wait_ge(mix_own, START + (b - 1) * MIX_OPS)
                        for t in range(T):
                            nc.scalar.activation(first[p][:, t, :], y[p][:, t, 0, :], ACT.Copy,
                                                 scale=one(weight, b * T + t)[:, 0:1]).then_inc(first_done, 1)

                    pipeline(eng, B, [(batch, 0)])

                @block.vector
                def _(eng):
                    def mix(b, p):
                        eng.wait_ge(first_done, START + (b + 1) * T)
                        eng.wait_ge(out_stored[p], (b - p) * 8)
                        for t in range(T):
                            eng.scalar_tensor_tensor(res[p][:, t, :], y[p][:, t, 1, :], one(weight, b * T + t)[:, 1:2],
                                                     first[p][:, t, :], ALU.mult, ALU.add).then_inc(mix_own, 1)
                        eng.wait_ge(mix_own, START + b * MIX_OPS + T)
                        gb = mod_row[:, bass.ds(b, 1), GB, :].to_broadcast([128, T, D])
                        eng.tensor_tensor(res[p][:], res[p][:], gb, ALU.mult).then_inc(mix_own, 1)
                        eng.wait_ge(mix_own, START + b * MIX_OPS + T + 1)
                        eng.tensor_tensor(res[p][:], res[p][:], X[:, bass.ds(b * T, T), :], ALU.add).then_inc(mix_own, 1)

                    pipeline(eng, B, [(mix, 0)])

                @block.gpsimd
                def _(eng):
                    def store(b, p):
                        eng.wait_ge(mix_own, START + (b + 1) * MIX_OPS)
                        eng.dma_start(out_rows[bass.ds(b * S, S), :].rearrange("(t p) d -> p t d", p=128), res[p][:]).then_inc(out_stored[p], 16)

                    pipeline(eng, B, [(store, 0)])
                    for p in (0, 1):
                        eng.wait_ge(out_stored[p], B // 2 * 16)


def kernel(L0_attn_x, L0_attn_Wq, L0_attn_Wk, L0_attn_Wv, L0_ffn_router_w, L0_ffn_w1, L0_ffn_b1, L0_ffn_w2, L0_ffn_b2,
           L0_c, L0_wmod):
    import ml_dtypes
    import numpy as np
    from concourse import bacc
    from concourse.bass_utils import run_bass_kernel_spmd

    def laid(a, *axes):
        a = np.asarray(a)
        return np.ascontiguousarray(a.transpose(axes) if axes else a)

    shift_rows = np.zeros((DK, S), ml_dtypes.bfloat16)
    shift_rows[0] = 1
    constants = np.zeros((128, CONSTS), np.float32)
    constants[:, 0:128] = np.eye(128)
    constants[:, 128:256] = np.triu(np.ones((128, 128)), 1)
    constants[:, 256:384] = 1
    constants[:, 384:512] = np.arange(128)
    constants[:, 512:512 + E] = np.arange(-E, 0)
    constants[:, 512 + E:512 + E + NT] = np.arange(1, NT + 1)
    constants[:, 512 + E + NT:512 + E + NT + 2] = 2 * np.arange(128)[:, None] + np.arange(2)
    constants[:, -1] = 2 * B * S + 1 + np.arange(128)
    arrays = {
        "x": laid(L0_attn_x),
        "wq_t": laid(L0_attn_Wq, 1, 0),
        "wk_t": laid(L0_attn_Wk, 1, 0),
        "wv_t": laid(L0_attn_Wv, 1, 0),
        "router_t": laid(L0_ffn_router_w, 1, 0),
        "w1_t": laid(L0_ffn_w1, 2, 0, 1),
        "b1_t": laid(np.asarray(L0_ffn_b1).reshape(E, FC, 128), 2, 0, 1),
        "w2_t": laid(np.asarray(L0_ffn_w2).reshape(E, D, FC, 128), 3, 0, 2, 1),
        "b2": laid(L0_ffn_b2),
        "c_t": laid(L0_c, 1, 0),
        "wmod": laid(L0_wmod),
        "constants": constants,
        "shift_rows": shift_rows,
    }
    nc = bacc.Bacc("TRN2", target_bir_lowering=False, num_devices=1)
    args = [nc.dram_tensor(name, a.shape, mybir.dt.from_np(a.dtype), kind="ExternalInput").ap() for name, a in arrays.items()]
    out = nc.dram_tensor("out", (B, S, D), FP32, kind="ExternalOutput").ap()
    adaln_block(nc, *args, out)
    result = run_bass_kernel_spmd(nc, [arrays], core_ids=[0])
    return result.results[0]["out"]
```

```python
import concourse.bass as bass
from concourse import mybir
from contextlib import ExitStack

FP32 = mybir.dt.float32
BF16 = mybir.dt.bfloat16
I32 = mybir.dt.int32
ALU = mybir.AluOpType
ACT = mybir.ActivationFunctionType
AX = mybir.AxisListType

B, S, D = 8, 512, 128
NH, DK = 16, 8
T = S // 128
NT = B * T
E, F = 8, 512
FC = F // 128
TS = 128
NST = (2 * B * S + E * (TS - 1)) // TS
ROWS = NST * TS // 128
G = 4
NG = NH // G
SCALE = DK ** -0.5
EPS = 1e-5
QUAD = 32
MT = 8
CONSTS = 4 * 128 + E + NT + MT + 1

START = 64

SEMAPHORES = """
    xn_done xT_done hT_done proj_done hi_done rest_done mid_done lo_done v_set v_copied ring_full ring_used
    score_done exp_done pv_done att_out recip_done xn2_done cb_done xn_used h2T_done h2T_out route_done lT_out
    logit_done logit_out top_own gap_done share_done ranks_done from_ready w_copied xsT_done xsT_out up_done
    gelu_done down_done y_out x_arrived0 x_arrived1 x_arrived2 x_arrived3 batch_loaded0 batch_loaded1 stored0
    stored1 stored2 stored3 shift_loaded0 shift_loaded1 h_stored0 h_stored1 h_stored2 h_stored3 y_loaded0 y_loaded1
    y_loaded2 y_loaded3 out_stored0 out_stored1 out_stored2 out_stored3 c_loaded loaded experts_loaded passed
    dve_own silu_exp silu_done mod_own diag_done mod_out col_done row_done row_out const_set op_set rows_loaded
    stat_own var_done std_done var2_done std2_done rstd2_own max_split x1_own last_own seg_set marks_made tiled
    numbered marks_used first_done mix_own sum_done
"""
FROM_ZERO = "gathered0 gathered1 gathered2 gathered3 scattered0 scattered1 scattered2 scattered3"


class Chain:

    def __init__(self, eng, sem, at=0, passed=None):
        self.eng, self.sem, self.at, self.passed = eng, sem, at, passed

    def link(self, ins):
        ins.then_inc(self.sem, 1)
        self.at = self.at + 1
        self.eng.wait_ge(self.sem, START + self.at)
        if self.passed:
            self.eng.sem_inc(self.passed, 1)


def split_in_three(own, whole, rest, part):
    own.link(own.eng.tensor_copy(part[0], whole))
    own.link(own.eng.tensor_tensor(rest, whole, part[0], ALU.subtract))
    own.link(own.eng.tensor_copy(part[1], rest))
    own.link(own.eng.tensor_tensor(part[2], rest, part[1], ALU.subtract))


def pipeline(eng, count, stages, depth=2, lead=True):
    most = max(ahead for _, ahead in stages)
    for t in range(-most if lead else 0, 0):
        for stage, ahead in stages:
            if 0 <= t + ahead < count:
                stage(t + ahead, (t + ahead) % depth)
    turns = (count - most) // depth
    with eng.Fori(0, turns) as i:
        for step in range(depth):
            for stage, ahead in stages:
                stage(i * depth + (step + ahead), (step + ahead) % depth)
    for t in range(depth * turns, count):
        for stage, ahead in stages:
            if t + ahead < count:
                stage(t + ahead, (t + ahead) % depth)


def adaln_block(nc, x, wq_t, wk_t, wv_t, router_t, w1_t, b1_t, w2_t, b2, c_t, wmod, constants, shift_rows, out):
    q_parts = nc.dram_tensor("q_parts", (B, 3, DK, NH, S), BF16, kind="Internal").ap()
    k_parts = nc.dram_tensor("k_parts", (B, 3 * DK, S), BF16, kind="Internal").ap()
    v_cols = nc.dram_tensor("v_cols", (B, 128, T * QUAD), FP32, kind="Internal").ap()
    h_rows = nc.dram_tensor("h_rows", (B * S, D), FP32, kind="Internal").ap()
    y_rows = nc.dram_tensor("y_rows", (2 * B * S + NST * TS, D), FP32, kind="Internal").ap()
    out_rows = out.rearrange("b s d -> (b s) d")

    ctx = ExitStack()
    with ctx:
        def sb(name, shape, dt=FP32):
            return ctx.enter_context(nc.sbuf_tensor(name, shape, dt))

        semaphores = {name: ctx.enter_context(nc.semaphore(name)) for name in (SEMAPHORES + FROM_ZERO).split()}
        sem = semaphores.get

        X = sb("X", [128, NT, D])
        consts = sb("consts", [128, CONSTS])
        ident, before, ones = (consts[:, 128 * n:128 * (n + 1)] for n in range(3))
        line = consts[:, 384:512]
        to_end, tile_number = consts[:, 512:512 + E], line[:, 0:NST]
        tile_after = consts[:, 512 + E:512 + E + NT]
        rest_of = consts[:, 512 + E + NT:512 + E + NT + MT]
        past_end = consts[:, CONSTS - 1:]
        wq = sb("wq", [D, D])
        wk = sb("wk", [D, DK])
        wv = sb("wv", [D, DK])
        rw = sb("rw", [D, QUAD])
        wm = sb("wm", [D, 6 * D])
        W1 = sb("W1", [128, E, F + FC + D])
        W2 = sb("W2", [128, E, FC, D])
        cT = sb("cT", [D, B])
        siluT = sb("siluT", [D, B])
        sign = sb("sign", [D, 2, B])
        silu_den = sb("silu_den", [D, B])
        mod_T = sb("mod_T", [D, 6, B])
        mod_row = sb("mod_row", [128, B, 4, D])
        GA, SB, CB, GB = range(4)
        eps = sb("eps", [128, 1])
        zero = sb("zero", [128, 1])

        ps = ctx.enter_context(nc.psum_tensor("ps", [128, 8 * 512], FP32))

        def bank(n, count=1):
            return ps[:, 512 * n:512 * (n + count)]

        Q = [sb(f"Q{p}", [128, NH, S], BF16) for p in (0, 1)]
        K = [sb(f"K{p}", [128, 2, S], BF16) for p in (0, 1)]
        V = [sb(f"V{p}", [128, T, QUAD]) for p in (0, 1)]
        ln_stats = sb("ln_stats", [128, NT, 6])

        XC = 4
        LOADED = 4 * 16
        c_loaded, loaded, experts_loaded = sem("c_loaded"), sem("loaded"), sem("experts_loaded")
        x_arrived = [sem(f"x_arrived{c}") for c in range(XC)]
        passed, dve_own, silu_exp, silu_done = sem("passed"), sem("dve_own"), sem("silu_exp"), sem("silu_done")
        mod_own, diag_done = sem("mod_own"), sem("diag_done")
        mod_out = sem("mod_out")
        batch_loaded = [sem(f"batch_loaded{p}") for p in (0, 1)]
        col_done, row_done, row_out = sem("col_done"), sem("row_done"), sem("row_out")
        const_set, op_set, rows_loaded = sem("const_set"), sem("op_set"), sem("rows_loaded")
        stat_own, var_done, std_done = sem("stat_own"), sem("var_done"), sem("std_done")
        LOADS = 3 + 3 + 1

        def load_operands(eng, b, p):
            for blk in range(3):
                at = QUAD * blk
                eng.dma_start(Q[p][at:at + 3 * DK, :, :].rearrange("p h t -> p (h t)"),
                              q_parts[bass.ds(b, 1), blk, :, :, :].rearrange("a d h t -> d (a h t)").partition_broadcast(3)
                              ).then_inc(batch_loaded[p], 16)
                eng.dma_start(K[p][at:at + 3 * DK, :, :], k_parts[bass.ds(b, 1), :, :].rearrange("a p t -> p a t")
                              .to_broadcast([3 * DK, 2, S])).then_inc(batch_loaded[p], 16)
            eng.dma_start(V[p][:].rearrange("p t c -> p (t c)"),
                          v_cols[bass.ds(b, 1), :, :].rearrange("a p c -> (a p) c")).then_inc(batch_loaded[p], 16)

        def one(tensor, n):
            return tensor[:, bass.ds(n, 1), :].rearrange("p a d -> p (a d)")

        def row_stats(eng, b):
            for t in range(T):
                eng.bn_stats(one(ln_stats, b * T + t), one(X, b * T + t)).then_inc(stat_own, 1)

        def variances(own, tiles, mean, var):
            even, odd = ln_stats[:, tiles, 1], ln_stats[:, tiles, 4]
            mean, var, tmp = mean[:, tiles], var[:, tiles], ln_tmp[:, tiles]
            own.link(own.eng.tensor_tensor(tmp, even, odd, ALU.subtract))
            own.link(own.eng.tensor_tensor(mean, even, odd, ALU.add))
            own.link(own.eng.tensor_scalar(mean, mean, 0.5, None, ALU.mult))
            own.link(own.eng.tensor_tensor(tmp, tmp, tmp, ALU.mult))
            own.link(own.eng.tensor_tensor(var, ln_stats[:, tiles, 2], ln_stats[:, tiles, 5], ALU.add))
            own.link(own.eng.tensor_scalar(var, var, 1.0 / D, None, ALU.mult))
            own.link(own.eng.scalar_tensor_tensor(var, tmp, 0.25, var, ALU.mult, ALU.add))

        with nc.Block() as block:
            def start(eng, k, of):
                for name in SEMAPHORES.split()[k::of]:
                    eng.sem_inc(sem(name), START)

            @block.sync
            def _(eng):
                eng.dma_start(cT[:], c_t).then_inc(c_loaded, 16)
                eng.dma_start(wm[:], wmod).then_inc(c_loaded, 16)
                eng.dma_start(consts[:], constants).then_inc(loaded, 16)
                eng.dma_start(wq[:], wq_t).then_inc(loaded, 16)
                eng.dma_start(wk[:], wk_t).then_inc(loaded, 16)
                eng.dma_start(wv[:], wv_t).then_inc(loaded, 16)

            @block.scalar
            def _(eng):
                rows = x.rearrange("b (t p) d -> p (b t) d", p=128)
                for c, arrived in enumerate(x_arrived):
                    these = slice(c * NT // XC, (c + 1) * NT // XC)
                    eng.dma_start(X[:, these, :], rows[:, these, :]).then_inc(arrived, 16)

            @block.vector
            def _(eng):
                start(eng, 0, 3)

            @block.gpsimd
            def _(eng):
                start(eng, 1, 3)

            @block.tensor
            def _(eng):
                start(eng, 2, 3)

        ln_mean, ln_rstd, ln_tmp = (sb(n, [128, NT]) for n in ("ln_mean", "ln_rstd", "ln_tmp"))
        diag = sb("diag", [D, B, 4, D])
        EARLIER, LATER = slice(0, NT // 2), slice(NT // 2, NT)

        def arrived_stats(eng, tiles):
            for n in range(tiles.start, tiles.stop):
                if n % (NT // XC) == 0:
                    eng.wait_ge(x_arrived[n * XC // NT], START + 16)
                eng.bn_stats(ln_stats[:, n, :], X[:, n, :]).then_inc(stat_own, 1)
            eng.wait_ge(stat_own, START + tiles.stop)

        with nc.Block() as block:
            @block.sync
            def _(eng):
                eng.wait_ge(op_set, START + 3)
                eng.dma_start(rw[:, 0:E], router_t).then_inc(rows_loaded, 16)
                for p in (0, 1):
                    for blk in range(3):
                        eng.dma_start(K[p][QUAD * blk + 24:QUAD * blk + 32, 1, :], shift_rows).then_inc(rows_loaded, 16)
                eng.wait_ge(loaded, START + LOADED)
                eng.wait_ge(x_arrived[-1], START + 16)
                eng.dma_start(W1[:, :, 0:F], w1_t).then_inc(experts_loaded, 16)
                eng.dma_start(W1[:, :, F:F + FC], b1_t).then_inc(experts_loaded, 16)
                eng.dma_start(W2[:], w2_t).then_inc(experts_loaded, 16)
                eng.dma_start(W1[:, :, F + FC:], b2.partition_broadcast(128)).then_inc(experts_loaded, 16)

            @block.gpsimd
            def _(eng):
                for operand in (rw, K[0], K[1], Q[0]):
                    eng.memset(operand[:].bitcast(I32), 0).then_inc(op_set, 1)
                eng.wait_ge(mod_out, START + 1)
                own = Chain(eng, mod_own)
                scales, gates = mod_T[:, 1:5:3, :], mod_T[:, 2:6:3, :]
                own.link(eng.tensor_scalar(scales, scales, 1.0, None, ALU.add))
                own.link(eng.tensor_scalar(sign[:], gates, 0.0, 2.0, ALU.is_ge, ALU.mult))
                own.link(eng.tensor_scalar(sign[:], sign[:], -1.0, None, ALU.add))
                own.link(eng.tensor_tensor(gates, gates, sign[:], ALU.mult))
                own.link(eng.tensor_scalar(gates, gates, 0.25, None, ALU.max))
                own.link(eng.tensor_tensor(gates, gates, sign[:], ALU.mult))

            @block.scalar
            def _(eng):
                eng.wait_ge(c_loaded, START + 32)
                eng.wait_ge(const_set, START + 2)
                nc.scalar.activation(silu_den[:], cT[:], ACT.Exp, bias=zero[:], scale=-1.0).then_inc(silu_exp, 1)
                eng.wait_ge(col_done, START + 1)
                nc.scalar.copy(mod_T[:], bank(7)[:, 0:6 * B].rearrange("p (k b) -> p k b", k=6)).then_inc(mod_out, 1)
                nc.scalar.preload_act_table(ACT.Sqrt)
                eng.wait_ge(var_done, START + 7)
                nc.scalar.activation(ln_rstd[:, EARLIER], ln_rstd[:, EARLIER], ACT.Sqrt, bias=eps[:]).then_inc(std_done, 1)

            @block.vector
            def _(eng):
                own = Chain(eng, dve_own)
                eng.memset(eps[:], EPS).then_inc(const_set, 1)
                eng.memset(zero[:], 0.0).then_inc(const_set, 1)
                eng.wait_ge(silu_exp, START + 1)
                own.link(eng.tensor_scalar(silu_den[:], silu_den[:], 1.0, None, ALU.add))
                own.link(eng.reciprocal(silu_den[:], silu_den[:]))
                own.link(eng.tensor_tensor(siluT[:], silu_den[:], cT[:], ALU.mult))
                eng.sem_inc(silu_done, 1)
                arrived_stats(eng, EARLIER)
                variances(Chain(eng, var_done), EARLIER, ln_mean, ln_rstd)
                eng.wait_ge(std_done, START + 1)
                eng.reciprocal(ln_rstd[:, EARLIER], ln_rstd[:, EARLIER]).then_inc(var_done, 1)

            @block.tensor
            def _(eng):
                eng.wait_ge(c_loaded, START + 32)
                eng.wait_ge(silu_done, START + 1)
                for k in range(6):
                    ins = eng.matmul(bank(7)[:, k * B:(k + 1) * B], wm[:, D * k:D * (k + 1)], siluT[:], start=True, stop=True)
                ins.then_inc(col_done, 1)

        SETS = 4
        parts = [sb(f"parts{n}", [D, 2, 3, S], BF16) for n in range(SETS)]
        vcol = [sb(f"vcol{n}", [128, T, QUAD]) for n in range(SETS)]
        stored = [sem(f"stored{n}") for n in range(SETS)]
        STORES = 3 * 16

        with ExitStack() as c1:
            def sb1(name, shape, dt=FP32):
                return c1.enter_context(nc.sbuf_tensor(name, shape, dt))

            xn = [sb1(f"xn{p}", [128, T, D]) for p in (0, 1)]
            hT = [sb1(f"hT{p}", [D, S]) for p in (0, 1)]
            rest = [sb1(f"rest{p}", [D, 2, S]) for p in (0, 1)]
            xn_done, xT_done, hT_done, proj_done, hi_done, rest_done, mid_done, lo_done, v_set, v_copied = (
                sem(n) for n in ("xn_done", "xT_done", "hT_done", "proj_done", "hi_done", "rest_done", "mid_done", "lo_done", "v_set", "v_copied"))

            ROWS_OF = (D, DK)

            def projected(p, n):
                return bank(4 * p + 1 + n)[0:ROWS_OF[n], :]

            with nc.Block() as block:
                @block.vector
                def _(eng):
                    for n in range(SETS):
                        eng.memset(vcol[n][:], 0.0).then_inc(v_set, 1)
                    eng.wait_ge(v_set, START + SETS)
                    for n in range(SETS):
                        eng.memset(vcol[n][:, :, DK:DK + 1], 1.0).then_inc(v_set, 1)
                    eng.wait_ge(v_set, START + 2 * SETS)

                    def normalize(b, k):
                        p = k % 2
                        eng.wait_ge(xT_done, START + b - 1)
                        for t in range(T):
                            eng.tensor_scalar(xn[p][:, t, :], one(X, b * T + t), ln_mean[:, bass.ds(b * T + t, 1)],
                                              ln_rstd[:, bass.ds(b * T + t, 1)], ALU.subtract, ALU.mult).then_inc(xn_done, 1)

                    def take(b, k):
                        p = k % 2
                        eng.wait_ge(lo_done, START + (b - 1) * 2)
                        for n in (0, 1):
                            eng.wait_ge(hi_done, START + b * 2 + n + 1)
                            eng.tensor_tensor(rest[p][0:ROWS_OF[n], n, :], projected(p, n), parts[k][0:ROWS_OF[n], n, 0, :],
                                              ALU.subtract).then_inc(rest_done, 1)
                        eng.wait_ge(stored[k], START + (b - k) * (STORES // SETS))
                        eng.tensor_copy(vcol[k][:, :, 0:DK],
                                        bank(4 * p + 3)[:, 0:T * DK].rearrange("p (t d) -> p t d", t=T)).then_inc(v_copied, 1)

                    normalize(0, 0)
                    normalize(1, 1)
                    arrived_stats(eng, LATER)
                    variances(Chain(eng, var_done, 8), LATER, ln_mean, ln_rstd)
                    eng.wait_ge(std_done, START + 2)
                    eng.reciprocal(ln_rstd[:, LATER], ln_rstd[:, LATER]).then_inc(var_done, 1)
                    eng.wait_ge(var_done, START + 16)
                    pipeline(eng, B, [(normalize, 2), (take, 0)], SETS, lead=False)

                @block.scalar
                def _(eng):
                    def modulate(b, k):
                        p = k % 2
                        eng.wait_ge(xT_done, START + b + 1)
                        eng.wait_ge(proj_done, START + b - 1)
                        nc.scalar.activation(hT[p][:], bank(4 * p), ACT.Identity, bias=mod_T[:, 0, bass.ds(b, 1)],
                                             scale=mod_T[:, 1, bass.ds(b, 1)]).then_inc(hT_done, 1)

                    def hi(b, k):
                        p = k % 2
                        eng.wait_ge(proj_done, START + b + 1)
                        eng.wait_ge(stored[k], START + (b - k) * (STORES // SETS))
                        for n in (0, 1):
                            nc.scalar.copy(parts[k][0:ROWS_OF[n], n, 0, :], projected(p, n)).then_inc(hi_done, 1)

                    def mid(b, k):
                        p = k % 2
                        for n in (0, 1):
                            eng.wait_ge(rest_done, START + b * 2 + n + 1)
                            nc.scalar.copy(parts[k][0:ROWS_OF[n], n, 1, :], rest[p][0:ROWS_OF[n], n, :]).then_inc(mid_done, 1)

                    modulate(0, 0)
                    modulate(1, 1)
                    eng.wait_ge(var_done, START + 15)
                    nc.scalar.activation(ln_rstd[:, LATER], ln_rstd[:, LATER], ACT.Sqrt, bias=eps[:]).then_inc(std_done, 1)
                    hi(0, 0)
                    pipeline(eng, B, [(mid, 0), (modulate, 2), (hi, 1)], SETS, lead=False)

                @block.gpsimd
                def _(eng):
                    def lo(b, k):
                        p = k % 2
                        for n in (0, 1):
                            eng.wait_ge(mid_done, START + b * 2 + n + 1)
                            eng.tensor_tensor(parts[k][0:ROWS_OF[n], n, 2, :], rest[p][0:ROWS_OF[n], n, :],
                                              parts[k][0:ROWS_OF[n], n, 1, :], ALU.subtract).then_inc(lo_done, 1)

                    for b in range(0, B, 2):
                        shape = [D, 2, 4, D]
                        eng.tensor_tensor(diag[:, b:b + 2, :, :], ident[:, None, None, :].to_broadcast(shape),
                                          mod_T[:, 2:6, b:b + 2, None].rearrange("p k b o -> p b k o").to_broadcast(shape),
                                          ALU.mult).then_inc(diag_done, 1)
                    eng.memset(Q[1][:].bitcast(I32), 0).then_inc(op_set, 1)
                    pipeline(eng, B, [(lo, 0)], SETS)

                @block.tensor
                def _(eng):
                    def turn_rows(b, k):
                        p = k % 2
                        eng.wait_ge(xn_done, START + (b + 1) * T)
                        eng.wait_ge(hT_done, START + b - 1)
                        for t in range(T):
                            ins = eng.transpose(bank(4 * p)[:, 128 * t:128 * (t + 1)], xn[p][:, t, :], ident)
                        ins.then_inc(xT_done, 1)

                    def project(b, k):
                        p = k % 2
                        eng.wait_ge(hT_done, START + b + 1)
                        eng.wait_ge(rest_done, START + (b - 1) * 2)
                        eng.wait_ge(v_copied, START + b - 1)
                        eng.matmul(projected(p, 0), wq[:], hT[p][:], start=True, stop=True)
                        eng.matmul(projected(p, 1), wk[:], hT[p][:], start=True, stop=True)
                        for t in range(T):
                            ins = eng.matmul(bank(4 * p + 3)[:, DK * t:DK * (t + 1)], hT[p][:, 128 * t:128 * (t + 1)], wv[:],
                                             start=True, stop=True)
                        ins.then_inc(proj_done, 1)

                    pipeline(eng, B, [(turn_rows, 1), (project, 0)], SETS)

                @block.sync
                def _(eng):
                    def store(b, k):
                        eng.wait_ge(v_copied, START + b + 1)
                        eng.dma_start(v_cols[bass.ds(b, 1), :, :].rearrange("a p c -> (a p) c"),
                                      vcol[k][:].rearrange("p t c -> p (t c)")).then_inc(stored[k], 16)
                        eng.wait_ge(lo_done, START + (b + 1) * 2)
                        eng.dma_start(q_parts[bass.ds(b, 1), :, :, :, :].rearrange("a i d h t -> (a d h) i t"),
                                      parts[k][:, 0, :, :]).then_inc(stored[k], 16)
                        eng.dma_start(k_parts[bass.ds(b, 1), :, :].rearrange("a (i p) t -> p (a i) t", p=DK),
                                      parts[k][0:DK, 1, :, :]).then_inc(stored[k], 16)

                    for b in range(SETS):
                        store(b, b)
                    eng.wait_ge(op_set, START + 5)
                    eng.wait_ge(stored[0], START + STORES)
                    load_operands(eng, 0, 0)
                    with eng.Fori(1, B // SETS) as i:
                        for k in range(SETS):
                            store(i * SETS + k, k)
                    eng.wait_ge(rows_loaded, START + 7 * 16)

        mean2, rstd2, shift2 = (sb(n, [128, NT]) for n in ("mean2", "rstd2", "shift2"))
        zeros, segments = sb("zeros", [128, E]), sb("segments", [128, E, NT])
        EARLY, LATE = slice(0, (B - 1) * T), slice((B - 1) * T, NT)
        var2_done, std2_done, rstd2_own = sem("var2_done"), sem("std2_done"), sem("rstd2_own")

        def scale_and_shift(own, tiles):
            own.link(own.eng.reciprocal(rstd2[:, tiles], rstd2[:, tiles]))
            own.link(own.eng.scalar_tensor_tensor(shift2[:, tiles], mean2[:, tiles], -1.0, rstd2[:, tiles], ALU.mult, ALU.mult))

        att = [sb(f"att{p}", [128, T, D]) for p in (0, 1)]

        with ExitStack() as c2:
            def sb2(name, shape, dt=FP32):
                return c2.enter_context(nc.sbuf_tensor(name, shape, dt))

            P = [sb2(f"P{p}", [128, G, S]) for p in (0, 1)]
            neg_max = [sb2(f"neg_max{p}", [128, G * T]) for p in (0, 1)]
            neg_max_T = [sb2(f"neg_max_T{p}", [G * T, 128]) for p in (0, 1)]
            max_rest = [sb2(f"max_rest{p}", [G * T, 128]) for p in (0, 1)]
            max_parts = [sb2(f"max_parts{p}", [G * T, 3, 128], BF16) for p in (0, 1)]
            att_u = [sb2(f"att_u{p}", [128, S]) for p in (0, 1)]
            recip = [sb2(f"recip{p}", [128, T, G]) for p in (0, 1)]
            gated = sb2("gated", [128, T, D])
            RING = 3
            FIRST = 2 * G * T + 1
            X1_OPS = T + 1
            GP = 2 * NG
            ring_full, ring_used, score_done, exp_done, pv_done, att_out, recip_done = (
                sem(n) for n in ("ring_full", "ring_used", "score_done", "exp_done", "pv_done", "att_out", "recip_done"))
            max_split, x1_own = sem("max_split"), sem("x1_own")
            shift_loaded = [sem(f"shift_loaded{p}") for p in (0, 1)]

            def ring_units(last):
                units = []
                for m in range(GP):
                    for s in range(T):
                        for j in range(G):
                            if not (last and m >= GP - 2):
                                units.append(("maximum", m + 2, s, j))
                            if s == 0 and j == 1 and not (last and m == GP - 1):
                                units.append(("maxima turned", m + 1))
                            if s == 2 and j == 1 and m > 0:
                                units.append(("sums turned", m - 1))
                return units + [("sums turned", GP - 1)]

            TURN = len(ring_units(False))
            assert TURN % RING == 0 and FIRST % RING == 0

            def ring_place(i, last, *unit):
                n = ring_units(last).index(unit)
                return i * TURN + (FIRST + n), bank(4 + n % RING)

            def start_place(*unit):
                units = [("maximum", 0, n // G, n % G) for n in range(G * T)] + [("maxima turned", 0)]
                units += [("maximum", 1, n // G, n % G) for n in range(G * T)]
                n = units.index(unit)
                return n, bank(4 + n % RING)

            with nc.Block() as block:
                @block.sync
                def _(eng):
                    def shift(n_split, m):
                        p, h = (m // NG) % 2, (m % NG) * G
                        eng.wait_ge(max_split, START + n_split)
                        for blk in range(3):
                            at = QUAD * blk + 24
                            eng.dma_start(Q[p][at:at + 1, h:h + G, :], max_parts[m % 2][:, blk, :]).then_inc(shift_loaded[m % 2], 16)

                    def turn(i, last):
                        for m in range(GP):
                            if not (last and m == GP - 1):
                                shift((i * GP + m + 2) * 4, m + 1)
                            if m == NG and not last:
                                eng.wait_ge(pv_done, START + i * (GP * T) + NG * T)
                                load_operands(eng, i * 2 + 2, 0)
                            if m == GP - 1 and not last:
                                eng.wait_ge(pv_done, START + (i + 1) * (GP * T))
                                load_operands(eng, i * 2 + 3, 1)

                    shift(4, 0)
                    for k in range(SETS):
                        eng.wait_ge(stored[k], START + B // SETS * STORES)
                    load_operands(eng, 1, 1)
                    with eng.Fori(0, B // 2 - 1) as i:
                        turn(i, False)
                    turn(B // 2 - 1, True)

                @block.tensor
                def _(eng):
                    def maximum(place, m, s, j):
                        eng.wait_ge(ring_used, START + place[0] - 2)
                        eng.matmul(place[1], Q[(m // NG) % 2][:, (m % NG) * G + j, 128 * s:128 * (s + 1)],
                                   K[(m // NG) % 2][:, 0, :], start=True, stop=True).then_inc(ring_full, 1)

                    def turn_maxima(place, m, before):
                        eng.wait_ge(ring_used, START + place[0] - before)
                        eng.transpose(place[1][0:G * T, 0:128], neg_max[m % 2][:], ident).then_inc(ring_full, 1)

                    def scores(i, m, s, u):
                        p = (m // NG) % 2
                        if s == 0 and u == 0:
                            eng.wait_ge(shift_loaded[m % 2], START + (i * (GP // 2) + m // 2 + 1) * 48)
                        eng.wait_ge(exp_done, START + i * (GP * T * 2) + (m * T + s) * 2 + u - 1)
                        for j in range(2):
                            ins = eng.matmul(bank(2 * u + j), K[p][:, 1, 128 * s:128 * (s + 1)], Q[p][:, (m % NG) * G + 2 * u + j, :],
                                             start=True, stop=True)
                        ins.then_inc(score_done, 1)

                    def values(i, m, s, heads):
                        if s == 0 and heads[0] == 0:
                            eng.wait_ge(att_out, START + i * GP + m)
                        for j in heads:
                            if j % 2 == 0:
                                eng.wait_ge(exp_done, START + i * (GP * T * 2) + (m * T + s) * 2 + j // 2 + 1)
                            ins = eng.matmul(bank(7)[QUAD * j:QUAD * (j + 1), :], V[(m // NG) % 2][:, s, :], P[s % 2][:, j, :],
                                             start=(s == 0), stop=(s == T - 1), tile_position=(0, QUAD * j))
                        if heads[-1] == G - 1:
                            ins.then_inc(pv_done, 1)

                    def back(place, i, m):
                        eng.wait_ge(att_out, START + i * GP + m + 1)
                        eng.wait_ge(ring_used, START + place[0] - 2)
                        for t in range(T):
                            ins = eng.transpose(place[1][:, 128 * t:128 * (t + 1)], att_u[m % 2][:, 128 * t:128 * (t + 1)], ident)
                        ins.then_inc(ring_full, 1)

                    def turn(i, last):
                        for m in range(GP):
                            for s in range(T):
                                ahead = not (last and m >= GP - 2)
                                if ahead and m == NG - 2 and s == 0:
                                    eng.wait_ge(batch_loaded[1], START + (i + 1) * (16 * LOADS))
                                if ahead and m == GP - 2 and s == 0:
                                    eng.wait_ge(batch_loaded[0], START + (i + 2) * (16 * LOADS))
                                for j in range(G):
                                    if ahead:
                                        maximum(ring_place(i, last, "maximum", m + 2, s, j), m + 2, s, j)
                                    if j % 2 == 0:
                                        scores(i, m, s, j // 2)
                                    elif s > 0:
                                        values(i, m, s - 1, (j - 1, j))
                                    elif m > 0 and j == 1:
                                        values(i, m - 1, T - 1, range(G))
                                    if s == 0 and j == 1 and not (last and m == GP - 1):
                                        turn_maxima(ring_place(i, last, "maxima turned", m + 1), m + 1, 2 if ahead else 0)
                                    if s == 2 and j == 1 and m > 0:
                                        back(ring_place(i, last, "sums turned", m - 1), i, m - 1)
                        values(i, GP - 1, T - 1, range(G))
                        back(ring_place(i, last, "sums turned", GP - 1), i, GP - 1)

                    def modulation_row(b):
                        eng.wait_ge(row_out, START + b - 3)
                        eng.matmul(bank(b % 4), ones, diag[:, b, :, :].rearrange("p k d -> p (k d)"), start=True, stop=True).then_inc(row_done, 1)

                    eng.wait_ge(batch_loaded[0], START + 16 * LOADS)
                    for m in (0, 1):
                        for n in range(G * T):
                            b = m * (G * T) + n - 8
                            if b >= 0 and b % 3 == 0 and b // 3 < B:
                                modulation_row(b // 3)
                            maximum(start_place("maximum", m, n // G, n % G), m, n // G, n % G)
                        if m == 0:
                            turn_maxima(start_place("maxima turned", 0), 0, 0)
                    eng.wait_ge(row_out, START + B)
                    with eng.Fori(0, B // 2 - 1) as i:
                        turn(i, False)
                    turn(B // 2 - 1, True)

                @block.scalar
                def _(eng):
                    def out_of_bank(i, m):
                        eng.wait_ge(pv_done, START + i * (GP * T) + (m + 1) * T)
                        nc.scalar.copy(att_u[m % 2][:], bank(7)).then_inc(att_out, 1)

                    def turn(i):
                        for m in range(GP):
                            for s in range(T):
                                eng.wait_ge(pv_done, START + i * (GP * T) + m * T + s - 1)
                                for u in range(2):
                                    eng.wait_ge(score_done, START + i * (GP * T * 2) + (m * T + s) * 2 + u + 1)
                                    nc.scalar.activation(P[s % 2][:, 2 * u:2 * u + 2, :],
                                                         bank(2 * u, 2).rearrange("p (j t) -> p j t", j=2),
                                                         ACT.Exp, bias=zero[:], scale=SCALE).then_inc(exp_done, 1)
                                    if s == 0 and u == 0 and m > 0:
                                        out_of_bank(i, m - 1)
                        out_of_bank(i, GP - 1)

                    nc.scalar.preload_act_table(ACT.Exp)
                    for b in range(B):
                        eng.wait_ge(row_done, START + b + 1)
                        nc.scalar.copy(mod_row[:, b, :, :].rearrange("p k d -> p (k d)"), bank(b % 4)).then_inc(row_out, 1)
                    with eng.Fori(0, B // 2) as i:
                        turn(i)
                    eng.wait_ge(var2_done, START + 7)
                    nc.scalar.activation(rstd2[:, EARLY], rstd2[:, EARLY], ACT.Sqrt, bias=eps[:]).then_inc(std2_done, 1)

                @block.vector
                def _(eng):
                    def take_maximum(place, m, s, j):
                        eng.wait_ge(ring_full, START + place[0] + 1)
                        eng.tensor_reduce(neg_max[m % 2][:, j * T + s:j * T + s + 1], place[1], AX.X, ALU.max,
                                          negate=True).then_inc(ring_used, 1)

                    def take_turned(place, n, m):
                        eng.wait_ge(ring_full, START + place[0] + 1)
                        eng.wait_ge(max_split, START + (n - 1) * 4)
                        eng.tensor_copy(neg_max_T[m % 2][:], place[1][0:G * T, 0:128]).then_inc(ring_used, 1)

                    def normalize(place, i, m):
                        p, g = m // NG, m % NG
                        sums = place[1].rearrange("p (t j c) -> p t j c", t=T, j=G)
                        eng.wait_ge(ring_full, START + place[0] + 1)
                        eng.reciprocal(recip[m % 2][:], sums[:, :, :, DK]).then_inc(recip_done, 1)
                        eng.wait_ge(recip_done, START + i * GP + m + 1)
                        if g == 0:
                            eng.wait_ge(x1_own, START + (i * 2 + p - 1) * X1_OPS)
                        eng.tensor_tensor(att[p][:, :, g * G * DK:(g + 1) * G * DK].rearrange("p t (j d) -> p t j d", j=G),
                                          sums[:, :, :, 0:DK],
                                          recip[m % 2][:, :, :, None].to_broadcast([128, T, G, DK]), ALU.mult).then_inc(ring_used, 1)

                    def turn(i, last):
                        for m in range(GP):
                            for s in range(T):
                                for j in range(G):
                                    if not (last and m >= GP - 2):
                                        take_maximum(ring_place(i, last, "maximum", m + 2, s, j), m + 2, s, j)
                                    if s == 0 and j == 1 and not (last and m == GP - 1):
                                        take_turned(ring_place(i, last, "maxima turned", m + 1), i * GP + m + 1, m + 1)
                                    if s == 2 and j == 1 and m > 0:
                                        normalize(ring_place(i, last, "sums turned", m - 1), i, m - 1)
                            if last and m == GP - 2:
                                eng.wait_ge(x1_own, START + (B - 1) * X1_OPS)
                                with eng.Fori(0, B - 1) as b:
                                    row_stats(eng, b)
                                eng.wait_ge(stat_own, START + NT + (B - 1) * T)
                                variances(Chain(eng, var2_done), EARLY, mean2, rstd2)
                        normalize(ring_place(i, last, "sums turned", GP - 1), i, GP - 1)

                    for m in (0, 1):
                        for n in range(G * T):
                            take_maximum(start_place("maximum", m, n // G, n % G), m, n // G, n % G)
                        if m == 0:
                            take_turned(start_place("maxima turned", 0), 0, 0)
                    with eng.Fori(0, B // 2 - 1) as i:
                        turn(i, False)
                    turn(B // 2 - 1, True)
                    eng.wait_ge(std2_done, START + 1)
                    scale_and_shift(Chain(eng, rstd2_own), EARLY)

                @block.gpsimd
                def _(eng):
                    def split(place, n, m):
                        p = m % 2
                        own = Chain(eng, max_split, n * 4, passed)
                        eng.wait_ge(ring_used, START + place[0] + 1)
                        eng.wait_ge(shift_loaded[p], START + (n - p) * 24)
                        eng.sem_inc(passed, 1)
                        split_in_three(own, neg_max_T[p][:], max_rest[p][:], [max_parts[p][:, part, :] for part in range(3)])

                    def add(place, i, p):
                        b = i * 2 + p
                        own = Chain(eng, x1_own, b * X1_OPS)
                        eng.wait_ge(ring_used, START + place[0] + 1)
                        for t in range(T):
                            ga = mod_row[:, bass.ds(b, 1), GA, :].rearrange("p a d -> p (a d)")
                            eng.tensor_tensor(gated[:, t, :], att[p][:, t, :], ga, ALU.mult).then_inc(x1_own, 1)
                        eng.wait_ge(x1_own, START + b * X1_OPS + T)
                        x1 = X[:, bass.ds(b * T, T), :]
                        eng.tensor_tensor(x1, x1, gated[:], ALU.add).then_inc(x1_own, 1)
                        eng.wait_ge(x1_own, START + (b + 1) * X1_OPS)

                    def turn(i, last):
                        for m in range(GP):
                            if not (last and m == GP - 1):
                                split(ring_place(i, last, "maxima turned", m + 1), i * GP + m + 1, m + 1)
                            if m == NG:
                                add(ring_place(i, last, "sums turned", NG - 1), i, 0)
                        if not last:
                            add(ring_place(i, last, "sums turned", GP - 1), i, 1)

                    split(start_place("maxima turned", 0), 0, 0)
                    eng.wait_ge(row_out, START + B)
                    with eng.Fori(0, B // 2 - 1) as i:
                        turn(i, False)
                    turn(B // 2 - 1, True)

        logits = sb("logits", [128, NT, E])
        hn = [sb(f"hn{k}", [128, T, D]) for k in range(SETS)]
        with ExitStack() as c3:
            def sb3(name, shape, dt=FP32):
                return c3.enter_context(nc.sbuf_tensor(name, shape, dt))

            xn = [sb3(f"r_xn{k}", [128, T, D]) for k in range(SETS)]
            hT = [sb3(f"r_hT{k}", [D, S]) for k in range(SETS)]
            lT = [sb3(f"r_lT{k}", [128, 128]) for k in range(SETS)]
            xn2_done, cb_done, xn_used, h2T_done, h2T_out, route_done, lT_out, logit_done, logit_out = (
                sem(n) for n in ("xn2_done", "cb_done", "xn_used", "h2T_done", "h2T_out",
                                 "route_done", "lT_out", "logit_done", "logit_out"))
            last_own, seg_set = sem("last_own"), sem("seg_set")
            h_stored = [sem(f"h_stored{k}") for k in range(SETS)]
            with nc.Block() as block:
                @block.vector
                def _(eng):
                    last, own = X[:, LATE, :], Chain(eng, last_own)
                    ga = mod_row[:, B - 1, None, GA, :].to_broadcast([128, T, D])
                    own.link(eng.tensor_tensor(att[(B - 1) % 2][:], att[(B - 1) % 2][:], ga, ALU.mult))
                    own.link(eng.tensor_tensor(last, last, att[(B - 1) % 2][:], ALU.add))
                    row_stats(eng, B - 1)
                    eng.wait_ge(stat_own, START + 2 * NT)
                    variances(Chain(eng, var2_done, 7), LATE, mean2, rstd2)

                    def modulate(b, k):
                        eng.wait_ge(xn2_done, START + (b + 1) * T)
                        cb = mod_row[:, bass.ds(b, 1), CB, :].to_broadcast([128, T, D])
                        eng.tensor_tensor(xn[k][:], xn[k][:], cb, ALU.mult).then_inc(cb_done, 1)

                    def turned(b, k):
                        eng.wait_ge(h2T_done, START + b + 1)
                        eng.wait_ge(route_done, START + b - 3)
                        eng.tensor_copy(hT[k][:], bank(4 * (k % 2))).then_inc(h2T_out, 1)

                    def out_of_bank(b, k):
                        eng.wait_ge(logit_done, START + b + 1)
                        eng.tensor_copy(logits[:, bass.ds(b * T, T), :],
                                        bank(4 * (k % 2) + 2)[:, 0:T * QUAD].rearrange("p (t e) -> p t e", t=T)[:, :, 0:E]).then_inc(logit_out, 1)

                    modulate(0, 0)
                    eng.wait_ge(std2_done, START + 2)
                    scale_and_shift(Chain(eng, rstd2_own, 2), LATE)
                    modulate(1, 1)
                    turned(0, 0)
                    modulate(2, 2)
                    turned(1, 1)
                    pipeline(eng, B, [(modulate, 3), (turned, 2), (out_of_bank, 0)], SETS, lead=False)

                @block.gpsimd
                def _(eng):
                    eng.memset(zeros[:], 0.0).then_inc(seg_set, 1)
                    eng.memset(segments[:], 1.0).then_inc(seg_set, 1)
                    eng.wait_ge(seg_set, START + 2)
                    eng.memset(segments[:, :, 0], 0.0).then_inc(seg_set, 1)

                    def batch(b, k):
                        sbias = mod_row[:, bass.ds(b, 1), SB, :].to_broadcast([128, T, D])
                        eng.wait_ge(cb_done, START + b + 1)
                        eng.wait_ge(h2T_done, START + b - 3)
                        eng.wait_ge(h_stored[k], START + (b - k) * (16 // SETS))
                        eng.tensor_tensor(hn[k][:], xn[k][:], sbias, ALU.add).then_inc(xn_used, 1)

                    pipeline(eng, B, [(batch, 0)], SETS)

                @block.sync
                def _(eng):
                    def batch(b, k):
                        eng.wait_ge(xn_used, START + b + 1)
                        eng.dma_start(h_rows[bass.ds(b * S, S), :].rearrange("(t p) d -> p t d", p=128), hn[k][:]).then_inc(h_stored[k], 16)

                    pipeline(eng, B, [(batch, 0)], SETS)

                @block.scalar
                def _(eng):
                    def normalize(b, k):
                        eng.wait_ge(xn_used, START + b - 3)
                        for t in range(T):
                            n = b * T + t
                            nc.scalar.activation(xn[k][:, t, :], one(X, n), ACT.Identity, bias=shift2[:, bass.ds(n, 1)],
                                                 scale=rstd2[:, bass.ds(n, 1)]).then_inc(xn2_done, 1)

                    def routed(b, k):
                        eng.wait_ge(route_done, START + b + 1)
                        eng.wait_ge(logit_done, START + b - 3)
                        nc.scalar.copy(lT[k][:], bank(4 * (k % 2) + 1)[:, 0:128]).then_inc(lT_out, 1)

                    normalize(0, 0)
                    normalize(1, 1)
                    eng.wait_ge(var2_done, START + 14)
                    nc.scalar.activation(rstd2[:, LATE], rstd2[:, LATE], ACT.Sqrt, bias=eps[:]).then_inc(std2_done, 1)
                    normalize(2, 2)
                    normalize(3, 3)
                    eng.wait_ge(rstd2_own, START + 4)
                    routed(0, 0)
                    pipeline(eng, B, [(normalize, 4), (routed, 1)], SETS, lead=False)

                @block.tensor
                def _(eng):
                    def turn_rows(b, k):
                        eng.wait_ge(xn_used, START + b + 1)
                        eng.wait_ge(h2T_out, START + b - 1)
                        for t in range(T):
                            ins = eng.transpose(bank(4 * (k % 2))[:, 128 * t:128 * (t + 1)], hn[k][:, t, :], ident)
                        ins.then_inc(h2T_done, 1)

                    def route(b, k):
                        eng.wait_ge(h2T_out, START + b + 1)
                        eng.wait_ge(lT_out, START + b - 1)
                        for t in range(T):
                            ins = eng.matmul(bank(4 * (k % 2) + 1)[QUAD * t:QUAD * (t + 1), 0:128], rw[:], hT[k][:, 128 * t:128 * (t + 1)],
                                             start=True, stop=True, tile_position=(0, QUAD * t))
                        ins.then_inc(route_done, 1)

                    def back(b, k):
                        eng.wait_ge(lT_out, START + b + 1)
                        eng.wait_ge(logit_out, START + b - 1)
                        eng.transpose(bank(4 * (k % 2) + 2)[:, 0:128], lT[k][:], ident).then_inc(logit_done, 1)

                    pipeline(eng, B, [(turn_rows, 2), (route, 1), (back, 0)], SETS)

        weight = sb("weight", [128, NT, 2])
        from_row = sb("from_row", [128, ROWS], I32)
        to_row = sb("to_row", [128, ROWS], I32)
        tile_expert = sb("tile_expert", [1, NST], I32)
        with ExitStack() as c4:
            def sb4(name, shape, dt=FP32):
                return c4.enter_context(nc.sbuf_tensor(name, shape, dt))

            best = sb4("best", [128, 2, NT])
            hot = sb4("hot", [128, 2, NT, E])
            masked = sb4("masked", [128, NT, E])
            work = sb4("work", [128, NT, E])
            index = sb4("index", [128, NT])
            chosen = sb4("chosen", [128, NT, E])
            total, upto = sb4("total", [128, E, NT]), sb4("upto", [128, E, NT])
            gap = sb4("gap", [128, NT])
            share = sb4("share", [128, NT])
            counts_i = sb4("counts_i", [128, E], I32)
            tiles = sb4("tiles", [128, E])
            tiles_to = sb4("tiles_to", [128, E])
            base = sb4("base", [128, E])
            beyond = sb4("beyond", [1, NST, E])
            expert_f = sb4("expert_f", [1, NST])
            place = sb4("place", [128, NT, 2])
            place_i = sb4("place_i", [128, NT, 2], I32)
            high = sb4("high", [128, NT, 2])
            is_low = [sb4(f"is_low{p}", [128, MT, 128], BF16) for p in (0, 1)]
            is_high = [sb4(f"is_high{p}", [128, MT, ROWS], BF16) for p in (0, 1)]
            by_high = [sb4(f"by_high{p}", [128, MT, 2, ROWS], BF16) for p in (0, 1)]
            found, found_rest = sb4("found", [128, ROWS]), sb4("found_rest", [128, ROWS])
            empty = sb4("empty", [128, ROWS])
            beside = sb4("beside", [128, ROWS])
            marks_made, tiled, numbered, marks_used = sem("marks_made"), sem("tiled"), sem("numbered"), sem("marks_used")

            MARKS = 2 * NT // MT
            low_part, high_part = (a[:].rearrange("p n c -> p (n c)") for a in (place, high))

            def choices(a, u):
                return a[:, bass.ds(u * MT, MT), None]

            top_own, gap_done, share_done, ranks_done = (sem(n) for n in ("top_own", "gap_done", "share_done", "ranks_done"))

            def over_experts(a):
                return a[:, :, None].to_broadcast([128, NT, E])

            def over_tiles(a):
                return a[:, None, :].to_broadcast([128, NT, E])

            with nc.Block() as block:
                @block.vector
                def _(eng):
                    own = Chain(eng, top_own)
                    for n in range(2):
                        hot_n, best_n, left = hot[:, n, :, :], best[:, n, :], (logits, masked)[n]
                        own.link(eng.tensor_reduce(best_n, left[:], AX.X, ALU.max))
                        own.link(eng.tensor_tensor(work[:], left[:], over_experts(best_n), ALU.is_equal))
                        own.link(eng.tensor_tensor(work[:], work[:], over_tiles(to_end), ALU.mult))
                        own.link(eng.tensor_reduce(index[:], work[:], AX.X, ALU.min))
                        own.link(eng.tensor_tensor(hot_n, over_tiles(to_end), over_experts(index[:]), ALU.is_equal))
                        if n == 0:
                            own.link(eng.scalar_tensor_tensor(masked[:], hot_n, -3.0e38, logits[:], ALU.mult, ALU.add))
                    eng.tensor_tensor(gap[:], best[:, 1, :], best[:, 0, :], ALU.subtract).then_inc(gap_done, 1)
                    own.link(eng.tensor_tensor(chosen[:], hot[:, 0, :, :], hot[:, 1, :, :], ALU.add))
                    eng.wait_ge(share_done, START + 1)
                    own.link(eng.tensor_scalar(gap[:], share[:], 1.0, None, ALU.add))
                    own.link(eng.reciprocal(weight[:, :, 0], gap[:]))
                    own.link(eng.tensor_tensor(weight[:, :, 1], weight[:, :, 0], share[:], ALU.mult))
                    eng.wait_ge(ranks_done, START + 2)
                    own.link(eng.tensor_copy(total[:], bank(1)[:, 0:NT * E].rearrange("p (n e) -> p e n", e=E)))
                    own.link(eng.tensor_tensor_scan(*(a[:].rearrange("p e n -> p (e n)") for a in (upto, segments, total)), 0.0,
                                                    ALU.mult, ALU.add))
                    own.link(eng.tensor_scalar(counts_i[:], upto[:, :, NT - 1], float(TS - 1), None, ALU.add))
                    own.link(eng.tensor_scalar(counts_i[:], counts_i[:], TS.bit_length() - 1, None, ALU.logical_shift_right))
                    own.link(eng.tensor_copy(tiles[:], counts_i[:]))
                    own.link(eng.tensor_tensor_scan(tiles_to[:], tiles[:], zeros[:], 0.0, ALU.add, ALU.add))
                    own.link(eng.tensor_tensor(base[:], tiles_to[:], tiles[:], ALU.subtract))
                    own.link(eng.tensor_scalar(base[:], base[:], float(TS), None, ALU.mult))
                    own.link(eng.tensor_tensor(work[:], upto[:].rearrange("p e n -> p n e"), total[:].rearrange("p e n -> p n e"), ALU.subtract))
                    own.link(eng.tensor_tensor(work[:], work[:], bank(0)[:, 0:NT * E].rearrange("p (n e) -> p n e", e=E), ALU.add))
                    own.link(eng.tensor_tensor(work[:], work[:], over_tiles(base[:]), ALU.add))
                    for n in range(2):
                        own.link(eng.tensor_tensor(masked[:], hot[:, n, :, :], work[:], ALU.mult))
                        own.link(eng.tensor_reduce(place[:, :, n], masked[:], AX.X, ALU.add))
                    own.link(eng.tensor_copy(place_i[:], place[:]))
                    own.link(eng.tensor_scalar(place_i[:], place_i[:], 7, None, ALU.logical_shift_right))
                    own.link(eng.tensor_copy(high[:], place_i[:]))
                    own.link(eng.scalar_tensor_tensor(place[:], high[:], -128.0, place[:], ALU.mult, ALU.add))

                    def marks(u, p):
                        eng.wait_ge(tiled, START + (u - 1) * (MT // 2))
                        eng.wait_ge(numbered, START + u - 1)
                        eng.tensor_tensor(is_high[p][:], line[:, None, 0:ROWS].to_broadcast([128, MT, ROWS]),
                                          choices(high_part, u).to_broadcast([128, MT, ROWS]), ALU.is_equal).then_inc(marks_made, 1)
                        eng.wait_ge(marks_used, START + u - 1)
                        eng.tensor_tensor(is_low[p][:], line[:, None, :].to_broadcast([128, MT, 128]),
                                          choices(low_part, u).to_broadcast([128, MT, 128]), ALU.is_equal).then_inc(marks_made, 1)

                    pipeline(eng, MARKS, [(marks, 0)])
                    own.link(eng.tensor_tensor(beyond[:], tile_number[0:1, :, None].to_broadcast([1, NST, E]),
                                               tiles_to[0:1, None, :].to_broadcast([1, NST, E]), ALU.is_ge))
                    own.link(eng.tensor_reduce(expert_f[:], beyond[:], AX.X, ALU.add))
                    own.link(eng.tensor_scalar(expert_f[:], expert_f[:], float(E - 1), None, ALU.min))
                    own.link(eng.tensor_copy(tile_expert[:], expert_f[:]))
                    own.link(eng.tensor_scalar(beside[:], line[:, 0:ROWS], 128.0, past_end, ALU.mult, ALU.add))
                    eng.wait_ge(marks_used, START + MARKS)
                    sums = bank(2)[:, 0:2 * ROWS].rearrange("p (a k) -> p a k", a=2)
                    own.link(eng.tensor_copy(found_rest[:], sums[:, 1, :]))
                    own.link(eng.scalar_tensor_tensor(found[:], sums[:, 0, :], 256.0, found_rest[:], ALU.mult, ALU.add))
                    own.link(eng.tensor_scalar(found[:], found[:], 1.0 - 256, 0.0, ALU.add, ALU.max))
                    own.link(eng.tensor_scalar(empty[:], found[:], 0.0, None, ALU.is_equal))
                    own.link(eng.tensor_tensor(empty[:], empty[:], beside[:], ALU.mult))
                    own.link(eng.scalar_tensor_tensor(to_row[:], found[:], -1.0, empty[:], ALU.add, ALU.add))
                    own.link(eng.tensor_scalar(from_row[:], found[:], 1.0, -1.0, ALU.max, ALU.add))
                    own.link(eng.tensor_scalar(from_row[:], from_row[:], 1, None, ALU.logical_shift_right))

                @block.scalar
                def _(eng):
                    nc.scalar.preload_act_table(ACT.Exp)
                    eng.wait_ge(gap_done, START + 1)
                    nc.scalar.activation(share[:], gap[:], ACT.Exp, bias=zero[:]).then_inc(share_done, 1)

                    def tiles_of(u, p):
                        eng.wait_ge(marks_made, START + u * 2 + 1)
                        eng.wait_ge(marks_used, START + u - 1)
                        for q in range(MT // 2):
                            nc.scalar.activation(by_high[p][:, 2 * q:2 * q + 2, 0, :], is_high[p][:, 2 * q:2 * q + 2, :], ACT.Copy,
                                                 scale=tile_after[:, bass.ds(u * (MT // 2) + q, 1)]).then_inc(tiled, 1)

                    pipeline(eng, MARKS, [(tiles_of, 0)])

                @block.tensor
                def _(eng):
                    eng.wait_ge(top_own, START + 5 + 1 + 5 + 1)
                    flat = chosen[:].rearrange("p n e -> p (n e)")
                    eng.matmul(bank(0)[:, 0:NT * E], before, flat, start=True, stop=True).then_inc(ranks_done, 1)
                    eng.matmul(bank(1)[:, 0:NT * E], ones, flat, start=True, stop=True).then_inc(ranks_done, 1)

                    def add_marks(u, p, first=False, final=False):
                        eng.wait_ge(marks_made, START + (u + 1) * 2)
                        eng.wait_ge(tiled, START + (u + 1) * (MT // 2))
                        eng.wait_ge(numbered, START + u + 1)
                        for k in range(MT):
                            ins = eng.matmul(bank(2)[:, 0:2 * ROWS], is_low[p][:, k, :], by_high[p][:, k, :, :].rearrange("p a k -> p (a k)"),
                                             start=first and k == 0, stop=final and k == MT - 1)
                        ins.then_inc(marks_used, 1)

                    add_marks(0, 0, first=True)
                    add_marks(1, 1)
                    with eng.Fori(1, MARKS // 2 - 1) as i:
                        add_marks(i * 2, 0)
                        add_marks(i * 2 + 1, 1)
                    add_marks(MARKS - 2, 0)
                    add_marks(MARKS - 1, 1, final=True)

                @block.gpsimd
                def _(eng):
                    def numbers(u, p):
                        eng.wait_ge(marks_made, START + u * 2 + 1)
                        eng.wait_ge(marks_used, START + u - 1)
                        eng.tensor_tensor(by_high[p][:, :, 1, :], is_high[p][:], rest_of[:, :, None].to_broadcast([128, MT, ROWS]),
                                          ALU.mult).then_inc(numbered, 1)

                    pipeline(eng, MARKS, [(numbers, 0)])

        with ExitStack() as c5:
            def sb5(name, shape, dt=FP32):
                return c5.enter_context(nc.sbuf_tensor(name, shape, dt))

            DEPTH = 4
            xs = [sb5(f"xs{p}", [128, D]) for p in range(DEPTH)]
            xsT = [sb5(f"xsT{p}", [D, TS]) for p in range(DEPTH)]
            from_now = [sb5(f"from_now{p}", [128, 1], I32) for p in range(DEPTH)]
            to_now = [sb5(f"to_now{p}", [128, 1], I32) for p in range(DEPTH)]
            w1_now = [sb5(f"w1_now{p}", [128, F + FC + D]) for p in range(DEPTH)]
            hid = [sb5(f"hid{p}", [128, FC, TS]) for p in range(DEPTH)]
            ys = [sb5(f"ys{p}", [128, D]) for p in range(DEPTH)]
            gathered = [sem(f"gathered{p}") for p in range(DEPTH)]
            scattered = [sem(f"scattered{p}") for p in range(DEPTH)]
            from_ready, w_copied, xsT_done, xsT_out, up_done, gelu_done, down_done, y_out = (
                sem(n) for n in ("from_ready", "w_copied", "xsT_done", "xsT_out", "up_done", "gelu_done", "down_done", "y_out"))

            def expert_of(eng, t):
                return eng.value_load(tile_expert[0:1, bass.ds(t, 1)], min_val=0, max_val=E - 1)

            with nc.Block() as block:
                @block.gpsimd
                def _(eng):
                    for k in range(SETS):
                        eng.wait_ge(h_stored[k], START + B // SETS * 16)

                    def gather(t, p):
                        eng.wait_ge(from_ready, START + t + 1)
                        eng.wait_ge(xsT_done, START + t - DEPTH + 1)
                        eng.sem_inc(passed, 1)
                        eng.indirect_dma_start(xs[p][:], None, h_rows,
                                               bass.IndirectOffsetOnAxis(ap=from_now[p][:], axis=0)).then_inc(gathered[p], 16)

                    def scatter(t, p):
                        eng.wait_ge(y_out, START + (t + 1) * 2)
                        eng.sem_inc(passed, 1)
                        eng.indirect_dma_start(y_rows, bass.IndirectOffsetOnAxis(ap=to_now[p][:], axis=0),
                                               ys[p][:], None).then_inc(scattered[p], 16)

                    pipeline(eng, NST, [(gather, 5), (scatter, 0)], DEPTH)
                    for p in range(DEPTH):
                        eng.wait_ge(scattered[p], (NST - p + DEPTH - 1) // DEPTH * 16)

                @block.vector
                def _(eng):
                    def where_from(t, p):
                        eng.wait_ge(xsT_done, START + t - DEPTH + 1)
                        eng.tensor_copy(from_now[p][:], from_row[:, bass.ds(t, 1)]).then_inc(from_ready, 1)

                    def weights(t, p):
                        e = expert_of(eng, t)
                        eng.wait_ge(up_done, START + t - DEPTH + 1)
                        eng.wait_ge(gelu_done, START + (t - DEPTH + 1) * FC)
                        eng.wait_ge(y_out, START + (t - DEPTH + 1) * 2)
                        eng.tensor_copy(w1_now[p][:], one(W1, e)).then_inc(w_copied, 1)

                    def transposed(t, p):
                        eng.wait_ge(xsT_done, START + t + 1)
                        eng.wait_ge(up_done, START + t - DEPTH + 1)
                        eng.tensor_copy(xsT[p][:], bank(4 + p % 2)[:, 0:TS]).then_inc(xsT_out, 1)

                    def results(t, p):
                        eng.wait_ge(scattered[p], (t - p) * (16 // DEPTH))
                        eng.tensor_copy(to_now[p][:], to_row[:, bass.ds(t, 1)]).then_inc(y_out, 1)
                        eng.wait_ge(down_done, START + t + 1)
                        eng.tensor_tensor(ys[p][:], bank(6 + p % 2)[:, 0:D], w1_now[p][:, F + FC:], ALU.add).then_inc(y_out, 1)

                    eng.wait_ge(experts_loaded, START + 4 * 16)
                    pipeline(eng, NST, [(transposed, 2), (where_from, 6), (weights, 3), (results, 0)], DEPTH)

                @block.scalar
                def _(eng):
                    def gelu(t, p):
                        eng.wait_ge(down_done, START + t - DEPTH + 1)
                        eng.wait_ge(up_done, START + t + 1)
                        for c in range(FC):
                            nc.scalar.activation(hid[p][:, c, :], bank(p)[:, TS * c:TS * (c + 1)], ACT.Gelu,
                                                 bias=w1_now[p][:, F + c:F + c + 1]).then_inc(gelu_done, 1)

                    nc.scalar.preload_act_table(ACT.Gelu)
                    pipeline(eng, NST, [(gelu, 0)], DEPTH)

                @block.tensor
                def _(eng):
                    def turn_rows(t, p):
                        eng.wait_ge(gathered[p], (t - p + DEPTH) * (16 // DEPTH))
                        eng.wait_ge(xsT_out, START + t - 1)
                        eng.transpose(bank(4 + p % 2)[:, 0:TS], xs[p][:], ident).then_inc(xsT_done, 1)

                    def up(t, p):
                        eng.wait_ge(w_copied, START + t + 1)
                        eng.wait_ge(xsT_out, START + t + 1)
                        eng.wait_ge(gelu_done, START + (t - DEPTH + 1) * FC)
                        for c in range(FC):
                            ins = eng.matmul(bank(p)[:, TS * c:TS * (c + 1)], w1_now[p][:, 128 * c:128 * (c + 1)], xsT[p][:],
                                             start=True, stop=True)
                        ins.then_inc(up_done, 1)

                    def down(t, p):
                        e = expert_of(eng, t)
                        eng.wait_ge(gelu_done, START + (t + 1) * FC)
                        eng.wait_ge(y_out, START + (t - 1) * 2)
                        for c in range(FC):
                            ins = eng.matmul(bank(6 + p % 2)[:, 0:D], hid[p][:, c, :], W2[:, bass.ds(e, 1), c, :].rearrange("p a d -> p (a d)"),
                                             start=(c == 0), stop=(c == FC - 1))
                        ins.then_inc(down_done, 1)

                    eng.wait_ge(experts_loaded, START + 4 * 16)
                    pipeline(eng, NST, [(turn_rows, 2), (up, 1), (down, 0)], DEPTH)

        with ExitStack() as c6:
            def sb6(name, shape, dt=FP32):
                return c6.enter_context(nc.sbuf_tensor(name, shape, dt))

            DEPTH = 4
            y = [sb6(f"y{p}", [128, T, 2, D]) for p in range(DEPTH)]
            first = [sb6(f"first{p}", [128, T, D]) for p in range(DEPTH)]
            res = [sb6(f"res{p}", [128, T, D]) for p in range(DEPTH)]
            first_done, mix_own, sum_done = sem("first_done"), sem("mix_own"), sem("sum_done")
            y_loaded = [sem(f"y_loaded{p}") for p in range(DEPTH)]
            out_stored = [sem(f"out_stored{p}") for p in range(DEPTH)]
            MIX_OPS = T + 1
            with nc.Block() as block:
                @block.sync
                def _(eng):
                    def load(b, p):
                        eng.wait_ge(mix_own, START + (b - DEPTH + 1) * MIX_OPS)
                        eng.dma_start(y[p][:], y_rows[bass.ds(b * (2 * S), 2 * S), :].rearrange("(t p n) d -> p t n d", p=128, n=2)
                                      ).then_inc(y_loaded[p], 16)

                    def store(b, p):
                        eng.wait_ge(sum_done, START + b + 1)
                        eng.dma_start(out_rows[bass.ds(b * S, S), :].rearrange("(t p) d -> p t d", p=128), res[p][:]).then_inc(out_stored[p], 16)

                    pipeline(eng, B, [(load, DEPTH), (store, 0)], DEPTH)
                    for p in range(DEPTH):
                        eng.wait_ge(out_stored[p], START + B // DEPTH * 16)

                @block.scalar
                def _(eng):
                    def batch(b, p):
                        eng.wait_ge(y_loaded[p], START + (b - p + DEPTH) * (16 // DEPTH))
                        eng.wait_ge(mix_own, START + (b - DEPTH + 1) * MIX_OPS)
                        for t in range(T):
                            nc.scalar.activation(first[p][:, t, :], y[p][:, t, 0, :], ACT.Copy,
                                                 scale=one(weight, b * T + t)[:, 0:1]).then_inc(first_done, 1)

                    pipeline(eng, B, [(batch, 0)], DEPTH)

                @block.vector
                def _(eng):
                    def mix(b, p):
                        eng.wait_ge(first_done, START + (b + 1) * T)
                        eng.wait_ge(out_stored[p], START + (b - p) * (16 // DEPTH))
                        for t in range(T):
                            eng.scalar_tensor_tensor(res[p][:, t, :], y[p][:, t, 1, :], one(weight, b * T + t)[:, 1:2],
                                                     first[p][:, t, :], ALU.mult, ALU.add).then_inc(mix_own, 1)
                        eng.wait_ge(mix_own, START + b * MIX_OPS + T)
                        gb = mod_row[:, bass.ds(b, 1), GB, :].to_broadcast([128, T, D])
                        eng.tensor_tensor(res[p][:], res[p][:], gb, ALU.mult).then_inc(mix_own, 1)

                    pipeline(eng, B, [(mix, 0)], DEPTH)

                @block.gpsimd
                def _(eng):
                    def add(b, p):
                        eng.wait_ge(mix_own, START + (b + 1) * MIX_OPS)
                        eng.tensor_tensor(res[p][:], res[p][:], X[:, bass.ds(b * T, T), :], ALU.add).then_inc(sum_done, 1)

                    pipeline(eng, B, [(add, 0)], DEPTH)


def kernel(L0_attn_x, L0_attn_Wq, L0_attn_Wk, L0_attn_Wv, L0_ffn_router_w, L0_ffn_w1, L0_ffn_b1, L0_ffn_w2, L0_ffn_b2,
           L0_c, L0_wmod):
    import ml_dtypes
    import numpy as np
    from concourse import bacc
    from concourse.bass_utils import run_bass_kernel_spmd

    def laid(a, *axes):
        a = np.asarray(a)
        return np.ascontiguousarray(a.transpose(axes) if axes else a)

    shift_rows = np.zeros((DK, S), ml_dtypes.bfloat16)
    shift_rows[0] = 1
    constants = np.zeros((128, CONSTS), np.float32)
    constants[:, 0:128] = np.eye(128)
    constants[:, 128:256] = np.triu(np.ones((128, 128)), 1)
    constants[:, 256:384] = 1
    constants[:, 384:512] = np.arange(128)
    constants[:, 512:512 + E] = np.arange(-E, 0)
    constants[:, 512 + E:512 + E + NT] = np.arange(1, NT + 1)
    constants[:, 512 + E + NT:512 + E + NT + MT] = 2 * np.arange(128)[:, None] + np.arange(MT) % 2
    constants[:, -1] = 2 * B * S + 1 + np.arange(128)
    arrays = {
        "x": laid(L0_attn_x),
        "wq_t": laid(np.asarray(L0_attn_Wq).reshape(NH, DK, D), 2, 1, 0).reshape(D, D),
        "wk_t": laid(L0_attn_Wk, 1, 0),
        "wv_t": laid(L0_attn_Wv, 1, 0),
        "router_t": laid(L0_ffn_router_w, 1, 0),
        "w1_t": laid(L0_ffn_w1, 2, 0, 1),
        "b1_t": laid(np.asarray(L0_ffn_b1).reshape(E, FC, 128), 2, 0, 1),
        "w2_t": laid(np.asarray(L0_ffn_w2).reshape(E, D, FC, 128), 3, 0, 2, 1),
        "b2": laid(L0_ffn_b2),
        "c_t": laid(L0_c, 1, 0),
        "wmod": laid(L0_wmod),
        "constants": constants,
        "shift_rows": shift_rows,
    }
    nc = bacc.Bacc("TRN2", target_bir_lowering=False, num_devices=1)
    args = [nc.dram_tensor(name, a.shape, mybir.dt.from_np(a.dtype), kind="ExternalInput").ap() for name, a in arrays.items()]
    out = nc.dram_tensor("out", (B, S, D), FP32, kind="ExternalOutput").ap()
    adaln_block(nc, *args, out)
    result = run_bass_kernel_spmd(nc, [arrays], core_ids=[0])
    return result.results[0]["out"]
```
